# Optimizing a Trainium2 kernel written in Bass

```python
import numpy as np
import jax
import jax.numpy as jnp

def _softmax(x, axis=-1):
    return jax.nn.softmax(x, axis=axis)

def _gelu(x):
    return jax.nn.gelu(x, approximate=True)

def _silu(x):
    return jax.nn.silu(x)

def _sigmoid(x):
    return jax.nn.sigmoid(x)

def _layernorm(x, axis=-1, eps=1e-05):
    m = jnp.mean(x, axis=axis, keepdims=True)
    v = jnp.var(x, axis=axis, keepdims=True)
    return (x - m) / jnp.sqrt(v + eps)

def _scatter_add(tgt, idx, src, axis=0):
    return tgt.at[idx].add(src)

def _segment_sum(src, seg, n):
    return jax.ops.segment_sum(src, seg, n)
kernel_name = 'mk_sandwich_d1_jaxref_r8_3af31e'

def setup_inputs(seed: int=0):
    np.random.seed(seed)
    _w = jnp.asarray

    def _L0_attn_setup():
        import jax, jax.numpy as jnp
        import numpy as np
        from jax import lax
        B, N, DIM = (2, 256, 128)
        HEADS, DHEAD = (16, 64)
        NUM_MEM_KV = 16
        SPARSE_TOPK = 64
        INNER = HEADS * DHEAD
        key = jax.random.key(seed)
        ks = jax.random.split(key, 10)
        s = 0.02
        return {'x': jax.random.normal(ks[0], (B, N, DIM), dtype=jnp.float32), 'Wq': jax.random.normal(ks[1], (DIM, INNER), dtype=jnp.float32) * s, 'Wk': jax.random.normal(ks[2], (DIM, INNER), dtype=jnp.float32) * s, 'Wv': jax.random.normal(ks[3], (DIM, INNER), dtype=jnp.float32) * s, 'pre_proj': jax.random.normal(ks[4], (HEADS, HEADS), dtype=jnp.float32), 'post_proj': jax.random.normal(ks[5], (HEADS, HEADS), dtype=jnp.float32), 'mem_k': jax.random.normal(ks[6], (HEADS, NUM_MEM_KV, DHEAD), dtype=jnp.float32), 'mem_v': jax.random.normal(ks[7], (HEADS, NUM_MEM_KV, DHEAD), dtype=jnp.float32), 'Wo': jax.random.normal(ks[8], (INNER, DIM), dtype=jnp.float32) * s, 'bo': jnp.zeros((DIM,), dtype=jnp.float32)}
    _L0_attn_in = _L0_attn_setup()

    def _L0_ffn_setup():
        import jax, jax.numpy as jnp
        import numpy as np
        DIM = 128
        HIDDEN = 384
        SCALE = 1.0 / 127.0

        def _dequant(w_int, dtype):
            return w_int.astype(dtype) * jnp.asarray(SCALE, dtype)
        key = jax.random.key(seed)
        k_x, k_g, k_u, k_d = jax.random.split(key, 4)
        x = jax.random.normal(k_x, (4, 256, DIM), dtype=jnp.float32)
        w_gate = jax.random.randint(k_g, (HIDDEN, DIM), -127, 128, dtype=jnp.int32)
        w_up = jax.random.randint(k_u, (HIDDEN, DIM), -127, 128, dtype=jnp.int32)
        w_down = jax.random.randint(k_d, (DIM, HIDDEN), -127, 128, dtype=jnp.int32)
        return {'x': x, 'w_gate': w_gate, 'w_up': w_up, 'w_down': w_down}
    _L0_ffn_in = _L0_ffn_setup()
    _d = {'L0_attn_x': _L0_attn_in['x'], 'L0_attn_Wq': _L0_attn_in['Wq'], 'L0_attn_Wk': _L0_attn_in['Wk'], 'L0_attn_Wv': _L0_attn_in['Wv'], 'L0_attn_pre_proj': _L0_attn_in['pre_proj'], 'L0_attn_post_proj': _L0_attn_in['post_proj'], 'L0_attn_mem_k': _L0_attn_in['mem_k'], 'L0_attn_mem_v': _L0_attn_in['mem_v'], 'L0_attn_Wo': _L0_attn_in['Wo'], 'L0_attn_bo': _L0_attn_in['bo'], 'L0_ffn_w_gate': _L0_ffn_in['w_gate'], 'L0_ffn_w_up': _L0_ffn_in['w_up'], 'L0_ffn_w_down': _L0_ffn_in['w_down']}
    _x0 = _d['L0_attn_x']
    _d['L0_attn_x'] = jax.random.normal(jax.random.fold_in(jax.random.key(seed), 1), (16, 512, 128), dtype=_x0.dtype)
    del _x0
    return _d

def reference(L0_attn_x, L0_attn_Wq, L0_attn_Wk, L0_attn_Wv, L0_attn_pre_proj, L0_attn_post_proj, L0_attn_mem_k, L0_attn_mem_v, L0_attn_Wo, L0_attn_bo, L0_ffn_w_gate, L0_ffn_w_up, L0_ffn_w_down):

    def _L0_attn_ref(x, Wq, Wk, Wv, pre_proj, post_proj, mem_k, mem_v, Wo, bo):
        import jax, jax.numpy as jnp
        import numpy as np
        from jax import lax
        B, N, DIM = (2, 256, 128)
        HEADS, DHEAD = (16, 64)
        NUM_MEM_KV = 16
        SPARSE_TOPK = 64
        INNER = HEADS * DHEAD
        b, n, _ = x.shape
        h, m, d = mem_k.shape
        scale = d ** (-0.5)

        def split_heads(t):
            return t.reshape(b, n, h, d).transpose(0, 2, 1, 3)
        q = split_heads(x @ Wq)
        k = split_heads(x @ Wk)
        v = split_heads(x @ Wv)
        k = jnp.concatenate([jnp.broadcast_to(mem_k[None], (b, h, m, d)), k], axis=2)
        v = jnp.concatenate([jnp.broadcast_to(mem_v[None], (b, h, m, d)), v], axis=2)
        dots = jnp.einsum('bhid,bhjd->bhij', q, k) * scale
        neg = -jnp.finfo(dots.dtype).max
        dots = jnp.einsum('bhij,hk->bkij', dots, pre_proj)
        j = m + n
        ii = jnp.arange(n)[:, None]
        jj = jnp.arange(j)[None, :]
        causal = jj - m > ii
        dots = jnp.where(causal[None, None], neg, dots)
        top = lax.top_k(dots, SPARSE_TOPK)[0]
        vk = top[..., -1:]
        dots = jnp.where(dots < vk, neg, dots)
        attn = jax.nn.softmax(dots, axis=-1)
        attn = jnp.einsum('bhij,hk->bkij', attn, post_proj)
        out = jnp.einsum('bhij,bhjd->bhid', attn, v)
        out = out.transpose(0, 2, 1, 3).reshape(b, n, h * d)
        return out @ Wo + bo

    def _L0_ffn_ref(x, w_gate, w_up, w_down):
        import jax, jax.numpy as jnp
        import numpy as np
        DIM = 128
        HIDDEN = 384
        SCALE = 1.0 / 127.0

        def _dequant(w_int, dtype):
            return w_int.astype(dtype) * jnp.asarray(SCALE, dtype)
        wg = _dequant(w_gate, x.dtype)
        wu = _dequant(w_up, x.dtype)
        wd = _dequant(w_down, x.dtype)
        gate = jnp.einsum('bsd,hd->bsh', x, wg)
        up = jnp.einsum('bsd,hd->bsh', x, wu)
        h = jax.nn.silu(gate) * up
        return jnp.einsum('bsh,dh->bsd', h, wd)
    x = L0_attn_x
    x = x + _layernorm(_L0_attn_ref(_layernorm(x, axis=-1), L0_attn_Wq, L0_attn_Wk, L0_attn_Wv, L0_attn_pre_proj, L0_attn_post_proj, L0_attn_mem_k, L0_attn_mem_v, L0_attn_Wo, L0_attn_bo), axis=-1)
    x = x + _layernorm(_L0_ffn_ref(_layernorm(x, axis=-1), L0_ffn_w_gate, L0_ffn_w_up, L0_ffn_w_down), axis=-1)
    return x

_drawn_inputs = setup_inputs


def setup_inputs(seed=0):
    import zlib

    import numpy as np

    out = dict(_drawn_inputs(seed))
    spreads = {'L0_attn_bo': (0.0, 0.1)}
    factors = {}
    for name, (base, spread) in spreads.items():
        noise = np.random.default_rng([zlib.crc32(name.encode()), seed]).standard_normal(out[name].shape)
        drawn = base * np.exp(spread * noise) if base else spread * noise
        out[name] = jnp.asarray(drawn.astype(out[name].dtype))
    for name, factor in factors.items():
        out[name] = (out[name] * factor).astype(out[name].dtype)
    return out
```

```python
from contextlib import ExitStack

import concourse.bass as bass
from concourse import mybir

F32 = mybir.dt.float32
BF16 = mybir.dt.bfloat16
I32 = mybir.dt.int32
ALU = mybir.AluOpType
ACT = mybir.ActivationFunctionType
AX_X = mybir.AxisListType.X

P = 128
B, N, D = 16, 512, 128
H, DH, M = 16, 64, 16
TOPK = 64
HID = 384
T = N // P
HC = HID // P
WC = H * DH // P
EPS = 1e-5
FMAX = 3.4028234663852886e38
MASKED = -2.0 ** 100

KEYS = [P * (t + 1) for t in range(T)]
ROW = [k + M for k in KEYS]
AT = [sum(ROW[:t]) for t in range(T)]
KEY_AT = [AT[t] + M * (t % 2) for t in range(T)]
WIDE = sum(ROW)
MEM_AT = KEYS[0]
ORDER = [3, 2, 1, 0]
RING = 8
ERING = 2
LAG_K = 4
LAG_P = 5
PEEL = 12

U_STEPS = {5: (0, 4), 6: (4, 7), 7: (7, 10), 8: (10, 13), 9: (13, 16)}
FFN_STEPS = {6: [("X1T",), ("GATE", 0), ("UP", 0)], 7: [("GATE", 1), ("UP", 1)],
             8: [("GATE", 2), ("UP", 2)], 10: [("DOWN",)]}


def misc_order(kind):
    uses = []
    if kind == "pro":
        return [("XT",)] + [("U", u) for u in range(16)]
    for s in range(PEEL):
        if kind != "drain":
            uses.append(("G", s))
            if s == 0:
                uses += [("MEM", 0), ("MEM", 1)]
        if s == 1 and kind in ("first", "mid"):
            uses.append(("XT",))
        if kind != "first":
            if s == 4:
                uses += [("PM", 0), ("PM", 1)]
            uses += FFN_STEPS.get(s, [])
        if kind in ("first", "mid") and s in U_STEPS:
            uses += [("U", u) for u in range(*U_STEPS[s])]
    if kind != "drain":
        uses += [("G", s) for s in range(PEEL, H)]
    return uses


KINDS = ("pro", "first", "mid", "last", "drain")
USES = {k: misc_order(k) for k in KINDS}
PLACE = {k: {u: i for i, u in enumerate(USES[k])} for k in KINDS}


def misc_index(kind, b, use):
    n = 0 if kind == "pro" else len(USES["pro"])
    if kind in ("mid", "last", "drain"):
        n += len(USES["first"])
    if kind == "mid":
        n = (b - 1) * len(USES["mid"]) + n
    if kind in ("last", "drain"):
        n += len(USES["mid"]) * (B - 2)
    if kind == "drain":
        n += len(USES["last"])
    if use[0] == "G" and not isinstance(use[1], int):
        return n + PLACE[kind][("G", PEEL)] - PEEL + use[1]
    return n + PLACE[kind][use]


def ln_index(kind, b, what):
    at = {"x": 0, "Y": 1, "X1": 2, "Z": 3}[what]
    if kind == "pro":
        return 0
    if kind == "first":
        return 1
    if kind == "mid":
        return (b - 1) * 4 + 2 + at
    return 2 + 4 * (B - 2) + (at - 1) + (3 if kind == "drain" else 0)


def batches(engine, body):
    body("first", 0)
    with engine.Fori(1, B - 1) as b:
        body("mid", b)
    body("last", B - 1)
    body("drain", B)


def steps(engine, kind, step):
    for s in range(PEEL):
        step(s)
    if kind != "drain":
        with engine.Fori(PEEL, H) as h:
            step(h)


def lagged(kind, s, lag):
    if not isinstance(s, int):
        return True
    return not (kind == "first" and s < lag) and not (kind == "drain" and s >= lag)


def head_of(s, lag):
    return (s - lag) % H if isinstance(s, int) else s - lag


def batch_of(b, s, lag):
    return b - 1 if isinstance(s, int) and s < lag else b


def at_least(engine, semaphore, value):
    if isinstance(value, int) and value <= 0:
        return
    engine.wait_ge(semaphore, value)


def alone(engine):
    engine.nop(nofuse=True)


def build(nc, x, wq, wk, wv, pre, post, memk, memv, wo, bo, wgate, wup, wdown, out):
    with ExitStack() as ctx:
        def sb(name, shape, dt=F32):
            return ctx.enter_context(nc.sbuf_tensor(name, shape, dt))

        def ps(name, shape):
            return ctx.enter_context(nc.psum_tensor(name, shape, F32))

        def sem(name):
            return ctx.enter_context(nc.semaphore(name))

        scores = sb("scores", [P, RING, WIDE])
        expo = sb("expo", [P, ERING, WIDE])
        work = sb("work", [P, WIDE])
        probs = sb("probs", [P, WIDE])
        probsT = sb("probsT", [P, 2, N])
        u_all = sb("u_all", [P, 2, T, H * D])
        a_all = sb("a_all", [P, H, D])
        b_all = sb("b_all", [P, H, D])
        amem = sb("amem", [P, H, M])
        umem = sb("umem", [P, 2, D])
        a_now = sb("a_now", [P, D])
        gT = sb("gT", [P, N])
        xcur = sb("xcur", [P, N])
        xnext = sb("xnext", [P, N])
        xwork = sb("xwork", [P, T, D])
        xres = sb("xres", [P, T, D])
        ybuf = sb("ybuf", [P, T, D])
        x1T = sb("x1T", [P, N])
        f_exp = sb("f_exp", [P, HC, N])
        f_gate = sb("f_gate", [P, HC, N])
        f_up = sb("f_up", [P, HC, N])
        wgT = sb("wgT", [P, HC, P])
        wuT = sb("wuT", [P, HC, P])
        wdT = sb("wdT", [P, HC, P])
        smem = sb("smem", [P, T, H, M])
        pmem = sb("pmem", [P, T, H, M])
        pmemT = sb("pmemT", [P, 2, N])
        causal = sb("causal", [P, P], BF16)
        ident16 = sb("ident16", [P, P], BF16)
        ident = sb("ident", [P, P])
        diag = sb("diag", [P, T, P])
        ones = sb("ones", [1, P])
        bo4 = sb("bo4", [1, T, D])
        memmax = sb("memmax", [P, T, H])
        rowmax = sb("rowmax", [P, RING, T])
        negmax = sb("negmax", [P, RING, T])
        kth = sb("kth", [P, RING, T])
        top8 = sb("top8", [P, T, 8])
        rowsum = sb("rowsum", [P, T])
        rinv = sb("rinv", [P, T])
        stats = sb("stats", [P, T, 6])
        meanvar = sb("meanvar", [P, T, 2])
        vareps = sb("vareps", [P, T])
        rstd = sb("rstd", [P, T])
        minus_half = sb("minus_half", [P, T])
        minus_one = sb("minus_one", [P, T])

        flat_u = u_all[:, :, :, :].rearrange("p a t n -> p (a t n)")
        take = [0]

        def cut(n):
            a = flat_u[:, take[0]:take[0] + n]
            take[0] += n
            return a

        wq_s, wk_s, wv_s = cut(WC * P), cut(WC * P), cut(WC * P)
        wqT = cut(WC * P).rearrange("p (c n) -> p c n", c=WC)
        wkT = cut(WC * (P + M)).rearrange("p (c n) -> p c n", c=WC)
        wvT = cut(WC * P).rearrange("p (c n) -> p c n", c=WC)
        mvT = cut(WC * M).rearrange("p (c n) -> p c n", c=WC)
        wo_s = cut(WC * D).rearrange("p (c n) -> p c n", c=WC)
        wk_mix = cut(2 * H * (P + M)).rearrange("p (a h n) -> p a h n", a=2, h=H)
        flat_s = scores[:, :, :].rearrange("p a n -> p (a n)")
        wo_mix = flat_s[:, 0:2 * H * D].rearrange("p (a h n) -> p a h n", a=2, h=H)
        umem_flat = flat_s[:, 2 * H * D:3 * H * D]
        mem_s = flat_s[:, 3 * H * D:3 * H * D + 512].rearrange("p (a g n) -> p a g n", a=2, g=2)
        flat_e = expo[:, :, :].rearrange("p a n -> p (a n)")
        pre_x = flat_e[:, 0:P].rearrange("p (c k) -> p c k", c=WC)
        post_x = flat_e[:, P:2 * P].rearrange("p (c h) -> p c h", c=WC)
        post_raw = flat_e[:, 2 * P:4 * P]
        w_int = flat_e[:, 4 * P:4 * P + 3 * HID].bitcast(I32).rearrange("p (a c n) -> p a c n", a=3, c=HC)
        w_f = f_exp[:, :, :].rearrange("p c n -> p (c n)")[:, 0:3 * HID].rearrange("p (a c n) -> p a c n", a=3, c=HC)

        s_bank = [ps(f"s_bank{i}", [P, N]) for i in range(4)]
        t_bank = [ps(f"t_bank{i}", [P, N]) for i in range(2)]
        y_bank = ps("y_bank", [P, N])
        misc = ps("misc", [P, N])

        w_in = sem("w_in")
        mix_in = sem("mix_in")
        x_in = sem("x_in")
        res_in = sem("res_in")
        out_sent = sem("out_sent")
        umem_in = sem("umem_in")
        ident_made = sem("ident_made")
        causal_made = sem("causal_made")
        consts_made = sem("consts_made")
        ffn_w_ready = sem("ffn_w_ready")
        turn_full = sem("turn_full")
        turn_taken = sem("turn_taken")
        post_spread = sem("post_spread")
        wk_mixed = sem("wk_mixed")
        wk_used = sem("wk_used")
        wo_mixed = sem("wo_mixed")
        wo_used = sem("wo_used")
        a_taken = sem("a_taken")
        b_taken = sem("b_taken")
        misc_full = sem("misc_full")
        misc_free = sem("misc_free")
        xcur_ready = sem("xcur_ready")
        a_ready = sem("a_ready")
        scores_full = sem("scores_full")
        masked = sem("masked")
        memmax_ready = sem("memmax_ready")
        mem_placed = sem("mem_placed")
        negmax_ready = sem("negmax_ready")
        exp_ready = sem("exp_ready")
        topk_step = sem("topk_step")
        kth_ready = sem("kth_ready")
        probs_ready = sem("probs_ready")
        rinv_ready = sem("rinv_ready")
        diag_ready = sem("diag_ready")
        pmem_ready = sem("pmem_ready")
        t_full = sem("t_full")
        t_taken = sem("t_taken")
        pv_done = sem("pv_done")
        y_full = sem("y_full")
        y_taken = sem("y_taken")
        ln_stats = sem("ln_stats")
        ln_meanvar = sem("ln_meanvar")
        ln_vareps = sem("ln_vareps")
        ln_rstd = sem("ln_rstd")
        ln_out = sem("ln_out")
        x1_ready = sem("x1_ready")
        out_ready = sem("out_ready")
        silu_pool = sem("silu_pool")
        silu_recip = sem("silu_recip")
        silu_ready = sem("silu_ready")

        x_t = x.rearrange("b (t p) d -> b p t d", p=P)
        out_t = out.rearrange("b (t p) d -> b p t d", p=P)
        banks = s_bank + t_bank + [y_bank, misc]

        def row(tensor, slot, t):
            return tensor[:, bass.ds(slot, 1), AT[t]:AT[t] + ROW[t]].squeeze(1)

        def keys(tensor, slot, t):
            return tensor[:, bass.ds(slot, 1), KEY_AT[t]:KEY_AT[t] + KEYS[t]].squeeze(1)

        def mem_parts(flat):
            return flat.rearrange("p (a c) -> p a c", a=2)[:, :, MEM_AT:MEM_AT + 2 * M].rearrange(
                "p a (t m) -> p a t m", t=2)

        def head_mem(tensor, h):
            return tensor[:, :, bass.ds(h, 1), :].rearrange("p (a t) h m -> p a t (h m)", a=2)

        def ring(g, size):
            return g % size

        turns = []
        for w_s in (wq_s, wk_s, wv_s):
            for half in range(2):
                turns.append([w_s[:, (4 * half + i) * P:(4 * half + i + 1) * P] for i in range(4)])
        for a in range(2):
            turns.append([mem_s[:, a, g, :] for g in range(2)])
        for a in range(3):
            turns.append([w_f[:, a, c, :] for c in range(HC)])

        block = ctx.enter_context(nc.Block())

        @block.sync
        def _(sp):
            sp.sem_inc(out_ready, 1)
            sp.sem_inc(silu_ready, 1)
            sp.sem_inc(out_sent, 16)
            sp.dma_start(wq_s, wq).then_inc(w_in, 16)
            sp.dma_start(wk_s, wk).then_inc(w_in, 16)
            sp.dma_start(wv_s, wv).then_inc(w_in, 16)
            for a, mem in enumerate((memk, memv)):
                for copy in range(2):
                    sp.dma_start(mem_s[:, a, :, copy * DH:(copy + 1) * DH],
                                 mem.rearrange("(g h) m c -> (h m) g c", g=2)).then_inc(w_in, 16)
            sp.dma_start(w_int[:, 0], wgate.rearrange("(c p) d -> p c d", p=P)).then_inc(w_in, 16)
            sp.dma_start(w_int[:, 1], wup.rearrange("(c p) d -> p c d", p=P)).then_inc(w_in, 16)
            sp.dma_start(w_int[:, 2], wdown.rearrange("p (c d) -> p c d", c=HC)).then_inc(w_in, 16)
            sp.dma_start(wo_s, wo.rearrange("(c p) o -> p c o", p=P)).then_inc(mix_in, 16)
            for half in range(2):
                src = pre.rearrange("(c a) k -> a c k", a=2)[half:half + 1]
                sp.dma_start(pre_x[half * DH:(half + 1) * DH], src.to_broadcast([DH, WC, H])).then_inc(mix_in, 16)
            sp.dma_start(post_raw, post.rearrange("(a h) k -> a (h k)", a=1).to_broadcast([P, H * H])).then_inc(mix_in, 16)
            sp.dma_start(xwork[:, :, :], x_t[0]).then_inc(x_in, 16)
            for t in range(T):
                sp.dma_start(bo4[0:1, t, :], bo.rearrange("(a d) -> a d", a=1)).then_inc(mix_in, 16)
            sp.wait_ge(b_taken, 8)
            for h in range(H):
                sp.dma_start(umem[M * (h % 8):M * (h % 8 + 1), h // 8, :],
                             umem_flat[0:M, h * D:(h + 1) * D]).then_inc(umem_in, 16)
            sp.wait_ge(misc_full, misc_index("pro", 0, ("XT",)) + 1)
            sp.dma_start(xwork[:, :, :], x_t[1]).then_inc(x_in, 16)

            def batch(kind, b):
                if kind != "first":
                    sp.wait_ge(out_ready, b)
                    sp.dma_start(xres[:, :, :], x_t[bass.ds(b - 1, 1)].squeeze(0)).then_inc(res_in, 16)
                if kind in ("first", "mid"):
                    last_use = ("XT",) if kind == "first" else ("X1T",)
                    sp.wait_ge(misc_full, misc_index(kind, b, last_use) + 1)
                    sp.dma_start(xwork[:, :, :], x_t[bass.ds((b + 2) % B, 1)].squeeze(0)).then_inc(x_in, 16)
                if kind != "first":
                    sp.wait_ge(out_ready, b + 1)
                    sp.dma_start(out_t[bass.ds(b - 1, 1)].squeeze(0), ybuf[:, :, :]).then_inc(out_sent, 16)

            batches(sp, batch)
            sp.wait_ge(out_sent, 16 * (B + 1))

        @block.tensor
        def _(pe):
            pe.wait_ge(ident_made, 2)
            pe.wait_ge(causal_made, 3)
            pe.wait_ge(w_in, 16 * 10)
            pe.wait_ge(consts_made, 3)
            for i, group in enumerate(turns):
                if i >= 8:
                    pe.wait_ge(turn_taken, i - 7)
                if i == 8:
                    pe.wait_ge(ffn_w_ready, 3)
                for j, src in enumerate(group):
                    mm = nc.tensor.transpose(banks[i % 8][:, j * P:(j + 1) * P], src, ident[:, :])
                mm.then_inc(turn_full, 1)
            pe.wait_ge(turn_taken, len(turns))
            for c in range(WC):
                pe.wait_ge(wk_mixed, c + 1)
                for q in range(4):
                    nc.tensor.matmul(banks[q][:, :], lhsT=wqT[:, c, :], rhs=wk_mix[:, c % 2, 4 * q:4 * q + 4, 0:P],
                                     start=(c == 0), stop=(c == WC - 1))
                nc.tensor.matmul(banks[4][:, 0:H * M], lhsT=wqT[:, c, :], rhs=wk_mix[:, c % 2, :, P:P + M],
                                 start=(c == 0), stop=(c == WC - 1)).then_inc(wk_used, 1)
            pe.wait_ge(a_taken, 5)
            for c in range(WC):
                pe.wait_ge(wo_mixed, c + 1)
                for q in range(4):
                    rhs = wo_mix[:, c % 2, 4 * q:4 * q + 4, :]
                    nc.tensor.matmul(banks[q][:, :], lhsT=wvT[:, c, :], rhs=rhs, start=(c == 0), stop=(c == WC - 1))
                    mm = nc.tensor.matmul(banks[4 + q][0:M, :], lhsT=mvT[:, c, :], rhs=rhs,
                                          start=(c == 0), stop=(c == WC - 1))
                mm.then_inc(wo_used, 1)
            pe.wait_ge(b_taken, 8)
            pe.wait_ge(umem_in, 16 * H)

            def share(kind, b, use):
                at_least(pe, misc_free, misc_index(kind, b, use))

            def turn_x(kind, b):
                pe.wait_ge(ln_out, 4 * (ln_index(kind, b, "x") + 1))
                share(kind, b, ("XT",))
                for t in range(T):
                    mm = nc.tensor.transpose(misc[:, t * P:(t + 1) * P], xwork[:, t, :], ident[:, :])
                mm.then_inc(misc_full, 1)

            def values(kind, b, u):
                share(kind, b, ("U", u))
                nc.tensor.matmul(misc[:, :], lhsT=xnext[:, (u // 4) * P:(u // 4 + 1) * P],
                                 rhs=b_all[:, 4 * (u % 4):4 * (u % 4) + 4, :], start=True, stop=True).then_inc(misc_full, 1)

            def start_y():
                nc.tensor.matmul(y_bank[:, :], lhsT=ones[:, :], rhs=bo4[:, :, :], start=True, stop=False,
                                 skip_group_check=True)

            turn_x("pro", 0)
            for u in range(16):
                values("pro", 0, u)
            start_y()

            def post(kind, b, s, g):
                h, par = head_of(s, LAG_P), batch_of(b, s, LAG_P) % 2
                pe.wait_ge(probs_ready, 4 * g + 4)
                pe.wait_ge(diag_ready, g + 1)

                def pv(p):
                    t, n = ORDER[p], 4 * g + p
                    pe.wait_ge(t_taken, n + 1)
                    for j in range(t + 1):
                        mm = nc.tensor.matmul(
                            y_bank[:, t * P:(t + 1) * P], lhsT=probsT[:, p % 2, j * P:(j + 1) * P],
                            rhs=u_all[:, bass.ds(par, 1), j, bass.ds(h * D, D)].squeeze(1),
                            start=False, stop=False, skip_group_check=True)
                    mm.then_inc(pv_done, 1)

                for p, t in enumerate(ORDER):
                    n = 4 * g + p
                    at_least(pe, t_taken, n - 1)
                    for j in range(t + 1):
                        mm = nc.tensor.matmul(t_bank[p % 2][:, j * P:(j + 1) * P],
                                              lhsT=probs[:, KEY_AT[t] + j * P:KEY_AT[t] + (j + 1) * P],
                                              rhs=diag[:, t, :], start=True, stop=True)
                    mm.then_inc(t_full, 1)
                    if p >= 1:
                        pv(p - 1)
                pv(3)

            def batch(kind, b):
                def step(s):
                    g = b * H + s
                    if kind != "drain":
                        if isinstance(s, int) and s == 0:
                            pe.wait_ge(xcur_ready, b + 1)
                        pe.wait_ge(a_ready, g + 1)
                        share(kind, b, ("G", s))
                        nc.tensor.matmul(misc[:, :], lhsT=a_now[:, :], rhs=xcur[:, :], start=True,
                                         stop=True).then_inc(misc_full, 1)
                        if isinstance(s, int) and s == 0:
                            for j in range(2):
                                share(kind, b, ("MEM", j))
                                for i in range(2):
                                    t = 2 * j + i
                                    mm = nc.tensor.matmul(misc[:, i * H * M:(i + 1) * H * M],
                                                          lhsT=xcur[:, t * P:(t + 1) * P], rhs=amem[:, :, :],
                                                          start=True, stop=True)
                                mm.then_inc(misc_full, 1)
                    if lagged(kind, s, LAG_P):
                        post(kind, b, s, g - LAG_P)
                    if kind != "drain":
                        pe.wait_ge(misc_free, misc_index(kind, b, ("G", s)) + 1)
                        for p, t in enumerate(ORDER):
                            n = 4 * g + p
                            at_least(pe, masked, n - 3)
                            nc.tensor.matmul(s_bank[p][:, 0:KEYS[t]], lhsT=gT[:, t * P:(t + 1) * P],
                                             rhs=xcur[:, 0:KEYS[t]], start=True, stop=False, skip_group_check=True)
                            nc.tensor.matmul(s_bank[p][:, t * P:(t + 1) * P], lhsT=ident16[:, :], rhs=causal[:, :],
                                             start=False, stop=True, skip_group_check=True).then_inc(scores_full, 1)
                    if not isinstance(s, int):
                        return
                    if s == 1 and kind in ("first", "mid"):
                        turn_x(kind, b)
                    if kind != "first" and s == 4:
                        pe.wait_ge(pmem_ready, b * H)
                        for j in range(2):
                            share(kind, b, ("PM", j))
                            for i in range(2):
                                for half in range(2):
                                    k = 2 * i + half
                                    mm = nc.tensor.transpose(misc[:, k * P:(k + 1) * P],
                                                             pmem[:, 2 * j + i, 8 * half:8 * half + 8, :], ident[:, :])
                            mm.then_inc(misc_full, 1)
                        pe.wait_ge(misc_free, misc_index(kind, b, ("PM", 1)) + 1)
                        for t in range(T):
                            for half in range(2):
                                k = 2 * (t % 2) + half
                                mm = nc.tensor.matmul(y_bank[:, t * P:(t + 1) * P],
                                                      lhsT=pmemT[:, t // 2, k * P:(k + 1) * P], rhs=umem[:, half, :],
                                                      start=False, stop=True, skip_group_check=True)
                        mm.then_inc(y_full, 1)
                        if kind != "drain":
                            pe.wait_ge(y_taken, b)
                            start_y()
                    if kind != "first":
                        for use in FFN_STEPS.get(s, []):
                            if use[0] == "X1T":
                                pe.wait_ge(ln_out, 4 * (ln_index(kind, b, "X1") + 1))
                            if use[0] == "DOWN":
                                pe.wait_ge(silu_ready, b + 1)
                            share(kind, b, use)
                            if use[0] == "X1T":
                                for t in range(T):
                                    mm = nc.tensor.transpose(misc[:, t * P:(t + 1) * P], xwork[:, t, :], ident[:, :])
                            elif use[0] == "DOWN":
                                for t in range(T):
                                    for c in range(HC):
                                        mm = nc.tensor.matmul(misc[:, t * P:(t + 1) * P],
                                                              lhsT=f_up[:, c, t * P:(t + 1) * P], rhs=wdT[:, c, :],
                                                              start=(c == 0), stop=(c == HC - 1))
                            else:
                                w = wgT if use[0] == "GATE" else wuT
                                mm = nc.tensor.matmul(misc[:, :], lhsT=w[:, use[1], :], rhs=x1T[:, :],
                                                      start=True, stop=True)
                            mm.then_inc(misc_full, 1)
                    if kind in ("first", "mid") and s in U_STEPS:
                        for u in range(*U_STEPS[s]):
                            values(kind, b, u)

                steps(pe, kind, step)

            batches(pe, batch)

        @block.scalar
        def _(act):
            taken = []
            for i, wT in enumerate((wqT, wkT, wvT)):
                for half in range(2):
                    taken.append([(wT[:, 4 * half:4 * half + 4, 0:P], None)])
            for i, mT in enumerate((wkT[:, :, P:P + M], mvT)):
                taken.append([(mT, i)])
            for wT in (wgT, wuT, wdT):
                taken.append([(wT[:, :, :], None)])
            for i, ((dst, mem),) in enumerate(taken):
                act.wait_ge(turn_full, i + 1)
                if mem is None:
                    n = dst.shape[1]
                    nc.scalar.copy(dst, banks[i % 8][:, 0:n * P].rearrange("p (c n) -> p c n", c=n)).then_inc(turn_taken, 1)
                else:
                    src = banks[i % 8][:, 0:H * M].rearrange("p (c a m) -> p c a m", a=2, m=M)
                    nc.scalar.copy(dst[0:DH], src[0:DH, :, 0, :])
                    nc.scalar.copy(dst[DH:P], src[DH:P, :, 1, :]).then_inc(turn_taken, 1)
            act.wait_ge(wk_used, WC)
            for q in range(4):
                nc.scalar.mul(a_all[:, 4 * q:4 * q + 4, :], banks[q][:, :].rearrange("p (h n) -> p h n", h=4),
                              DH ** -0.5).then_inc(a_taken, 1)
            nc.scalar.mul(amem[:, :, :], banks[4][:, 0:H * M].rearrange("p (h n) -> p h n", h=H),
                          DH ** -0.5).then_inc(a_taken, 1)
            act.wait_ge(wo_used, WC)
            for q in range(4):
                nc.scalar.copy(b_all[:, 4 * q:4 * q + 4, :],
                               banks[q][:, :].rearrange("p (h n) -> p h n", h=4)).then_inc(b_taken, 1)
            for q in range(4):
                nc.scalar.copy(umem_flat[0:M, q * 512:(q + 1) * 512], banks[4 + q][0:M, :]).then_inc(b_taken, 1)

            def take(kind, b, use, dst, src=None):
                act.wait_ge(misc_full, misc_index(kind, b, use) + 1)
                nc.scalar.copy(dst, misc[:, :] if src is None else src).then_inc(misc_free, 1)

            def take_values(kind, b, u, par):
                dst = u_all[:, bass.ds(par, 1), u // 4, 512 * (u % 4):512 * (u % 4 + 1)].squeeze(1)
                take(kind, b, ("U", u), dst)

            take("pro", 0, ("XT",), xnext[:, :])
            act.wait_ge(umem_in, 16 * H)
            for u in range(16):
                take_values("pro", 0, u, 0)

            def batch(kind, b):
                def step(s):
                    g = b * H + s
                    if kind != "drain":
                        if isinstance(s, int) and s == 0:
                            act.wait_ge(misc_free, misc_index("pro", 0, ("XT",)) + 1 if kind == "first" else
                                        misc_index("first", 0, ("XT",)) + 1)
                            at_least(act, scores_full, 4 * g)
                            nc.scalar.copy(xcur[:, :], xnext[:, :]).then_inc(xcur_ready, 1)
                        at_least(act, scores_full, 4 * g)
                        take(kind, b, ("G", s), gT[:, :])
                        if isinstance(s, int) and s == 0:
                            at_least(act, mem_placed, 16 * b)
                            at_least(act, memmax_ready, b)
                            for j in range(2):
                                take(kind, b, ("MEM", j), smem[:, 2 * j:2 * j + 2, :, :],
                                     misc[:, :].rearrange("p (t h m) -> p t h m", t=2, h=H))
                    if lagged(kind, s, LAG_K):
                        ge = g - LAG_K
                        act.wait_ge(masked, 4 * ge + 4)
                        act.wait_ge(mem_placed, ge + 1)
                        act.wait_ge(negmax_ready, ge + 1)
                        at_least(act, probs_ready, 4 * (ge - 1))
                        for t in ORDER:
                            nc.scalar.activation(row(expo, ring(head_of(s, LAG_K), ERING), t),
                                                 row(scores, ring(head_of(s, LAG_K), RING), t), ACT.Exp,
                                                 bias=negmax[:, bass.ds(ring(head_of(s, LAG_K), RING), 1), t]
                                                 ).then_inc(exp_ready, 1)
                    if lagged(kind, s, LAG_P):
                        gp = g - LAG_P
                        for p, t in enumerate(ORDER):
                            act.wait_ge(t_full, 4 * gp + p + 1)
                            at_least(act, pv_done, 4 * gp + p - 1)
                            nc.scalar.copy(probsT[:, p % 2, 0:KEYS[t]], t_bank[p % 2][:, 0:KEYS[t]]).then_inc(t_taken, 1)
                    if not isinstance(s, int):
                        return
                    if s == 1 and kind in ("first", "mid"):
                        take(kind, b, ("XT",), xnext[:, :])
                    if kind != "first" and s == 4:
                        for j in range(2):
                            take(kind, b, ("PM", j), pmemT[:, j, :])
                        act.wait_ge(y_full, b)
                        act.wait_ge(out_sent, 16 * b)
                        nc.scalar.copy(ybuf[:, :, :], y_bank[:, :].rearrange("p (t d) -> p t d", t=T)).then_inc(y_taken, 1)
                    if kind != "first":
                        for use in FFN_STEPS.get(s, []):
                            if use[0] == "X1T":
                                take(kind, b, use, x1T[:, :])
                            elif use[0] == "GATE":
                                act.wait_ge(silu_ready, b)
                                act.wait_ge(misc_full, misc_index(kind, b, use) + 1)
                                nc.scalar.activation(f_exp[:, use[1], :], misc[:, :], ACT.Exp, scale=-1.0)
                                nc.scalar.copy(f_gate[:, use[1], :], misc[:, :]).then_inc(misc_free, 1)
                            elif use[0] == "UP":
                                take(kind, b, use, f_up[:, use[1], :])
                            else:
                                take(kind, b, use, ybuf[:, :, :], misc[:, :].rearrange("p (t d) -> p t d", t=T))
                    if kind in ("first", "mid") and s in U_STEPS:
                        for u in range(*U_STEPS[s]):
                            take_values(kind, b, u, (b + 1) % 2)

                steps(act, kind, step)

            batches(act, batch)

        @block.vector
        def _(dve):
            nc.vector.memset(minus_half[:, :], -0.5).then_inc(consts_made, 1)
            nc.vector.memset(minus_one[:, :], -1.0).then_inc(consts_made, 1)
            nc.vector.memset(ones[:, :], 1.0).then_inc(consts_made, 1)
            dve.wait_ge(mix_in, 16 * (1 + 2 + 1 + T))
            for a in range(2):
                nc.vector.tensor_copy(post_x[a * DH:(a + 1) * DH], post_raw[a * DH:(a + 1) * DH].rearrange(
                    "p (h c a) -> p a c h", a=2, c=WC)[:, a]).then_inc(post_spread, 1)
            dve.wait_ge(w_in, 16 * 10)
            for a in range(3):
                nc.vector.tensor_scalar(w_f[:, a], w_int[:, a], 1.0 / 127.0, None, ALU.mult).then_inc(ffn_w_ready, 1)
            dve.wait_ge(turn_taken, 8)
            for c in range(WC):
                if c >= 2:
                    dve.wait_ge(wk_used, c - 1)
                nc.vector.tensor_tensor(wk_mix[:, c % 2], wkT[:, c, :].unsqueeze(1).to_broadcast([P, H, P + M]),
                                        pre_x[:, c, :].unsqueeze(2).to_broadcast([P, H, P + M]),
                                        ALU.mult).then_inc(wk_mixed, 1)

            def norm_stats(kind, b, what, src):
                n = ln_index(kind, b, what)
                for t in range(T):
                    nc.vector.bn_stats(stats[:, t, :], src[:, t, :]).then_inc(ln_stats, 1)
                dve.wait_ge(ln_stats, 4 * (n + 1))
                alone(dve)
                for t in range(T):
                    nc.vector.bn_aggr(meanvar[:, t, :], stats[:, t, :]).then_inc(ln_meanvar, 1)

            def norm_apply(kind, b, what, dst, src):
                n = ln_index(kind, b, what)
                dve.wait_ge(ln_rstd, n + 1)
                for t in range(T):
                    nc.vector.tensor_scalar(dst[:, t, :], src[:, t, :], meanvar[:, t, 0:1], rstd[:, t:t + 1],
                                            ALU.subtract, ALU.mult).then_inc(ln_out, 1)

            dve.wait_ge(x_in, 16)
            norm_stats("pro", 0, "x", xwork)
            norm_apply("pro", 0, "x", xwork, xwork)

            def batch(kind, b):
                def step(s):
                    g = b * H + s
                    fixed = isinstance(s, int)
                    if fixed and s == 0 and kind in ("first", "mid"):
                        dve.wait_ge(x_in, 16 * (b + 2))
                        norm_stats(kind, b, "x", xwork)
                    if fixed and s == 5 and kind != "first":
                        dve.wait_ge(y_taken, b)
                        norm_stats(kind, b, "Y", ybuf)
                    if fixed and s == 6 and kind != "first":
                        if kind != "drain" and kind != "last":
                            dve.wait_ge(misc_full, misc_index(kind, b, ("XT",)) + 1)
                        norm_apply(kind, b, "X1", xwork, xres)
                    if fixed and s == 11 and kind != "first":
                        dve.wait_ge(misc_free, misc_index(kind, b, ("DOWN",)) + 1)
                        norm_stats(kind, b, "Z", ybuf)
                    if lagged(kind, s, LAG_P):
                        gp = g - LAG_P
                        slot = ring(head_of(s, LAG_P), RING)
                        dve.wait_ge(exp_ready, 4 * gp + 4)
                        at_least(dve, t_full, 4 * gp)
                        at_least(dve, pmem_ready, gp)
                        at_least(dve, diag_ready, gp)
                        dve.wait_ge(kth_ready, gp + 1)
                        for t in ORDER:
                            nc.vector.scalar_tensor_tensor(
                                out=probs[:, AT[t]:AT[t] + ROW[t]], in0=row(scores, slot, t),
                                scalar=kth[:, bass.ds(slot, 1), t], in1=row(expo, ring(head_of(s, LAG_P), ERING), t),
                                op0=ALU.is_ge, op1=ALU.mult, accum_out=rowsum[:, t:t + 1]).then_inc(probs_ready, 1)
                        dve.wait_ge(probs_ready, 4 * gp + 4)
                        nc.vector.reciprocal(rinv[:, :], rowsum[:, :]).then_inc(rinv_ready, 1)
                    if lagged(kind, s, LAG_K):
                        gk = g - LAG_K
                        dve.wait_ge(mem_placed, gk + 1)
                        dve.wait_ge(masked, 4 * gk + 4)
                        slot = ring(head_of(s, LAG_K), RING)
                        for t in ORDER:
                            nc.vector.tensor_copy(work[:, AT[t]:AT[t] + ROW[t]], row(scores, slot, t)).then_inc(topk_step, 1)
                        for i in range(15):
                            for p, t in enumerate(ORDER):
                                wrk = work[:, AT[t]:AT[t] + ROW[t]]
                                dve.wait_ge(topk_step, T * i + p + 1)
                                if i % 2 == 0:
                                    nc.vector.max(top8[:, t, :], wrk).then_inc(topk_step, 1)
                                else:
                                    nc.vector.match_replace(wrk, top8[:, t, :], wrk, -FMAX).then_inc(topk_step, 1)
                        dve.wait_ge(topk_step, 16 * T)
                        dve.sem_clear(topk_step)
                        nc.vector.tensor_copy(kth[:, bass.ds(slot, 1), :].squeeze(1),
                                              top8[:, :, 7:8].squeeze(2)).then_inc(kth_ready, 1)
                    if fixed and s == 0 and kind != "drain":
                        dve.wait_ge(misc_free, misc_index(kind, b, ("MEM", 1)) + 1)
                        nc.vector.reduce_max(memmax[:, :, :].rearrange("p t h -> p (t h)"),
                                             smem[:, :, :, :].rearrange("p t h m -> p (t h) m"),
                                             AX_X).then_inc(memmax_ready, 1)
                    if kind != "drain":
                        if fixed and s == 0:
                            dve.wait_ge(memmax_ready, b + 1)
                        slot = ring(head_of(s, 0), RING)
                        for p, t in enumerate(ORDER):
                            dve.wait_ge(scores_full, 4 * g + p + 1)
                            nc.vector.tensor_scalar(keys(scores, slot, t), s_bank[p][:, 0:KEYS[t]], 1.0,
                                                    memmax[:, t, bass.ds(s, 1)], ALU.mult, ALU.max,
                                                    accum_out=rowmax[:, bass.ds(slot, 1), t]).then_inc(masked, 1)
                    if not fixed:
                        return
                    if s == 0 and kind in ("first", "mid"):
                        norm_apply(kind, b, "x", xwork, xwork)
                    if kind == "first":
                        return
                    if s == 5:
                        norm_apply(kind, b, "Y", ybuf, ybuf)
                        dve.wait_ge(res_in, 16 * b)
                        dve.wait_ge(ln_out, 4 * (ln_index(kind, b, "Y") + 1))
                        nc.vector.tensor_tensor(xres[:, :, :], xres[:, :, :], ybuf[:, :, :], ALU.add).then_inc(x1_ready, 1)
                        dve.wait_ge(x1_ready, b)
                        norm_stats(kind, b, "X1", xres)
                    if s == 9:
                        dve.wait_ge(silu_pool, 2 * b)
                        nc.vector.reciprocal(f_exp[:, :, :], f_exp[:, :, :]).then_inc(silu_recip, 1)
                        dve.wait_ge(silu_recip, b)
                        nc.vector.tensor_tensor(f_up[:, :, :], f_up[:, :, :], f_exp[:, :, :], ALU.mult).then_inc(silu_ready, 1)
                    if s == 11:
                        norm_apply(kind, b, "Z", ybuf, ybuf)
                        dve.wait_ge(ln_out, 4 * (ln_index(kind, b, "Z") + 1))
                        nc.vector.tensor_tensor(ybuf[:, :, :], xres[:, :, :], ybuf[:, :, :], ALU.add).then_inc(out_ready, 1)

                steps(dve, kind, step)

            batches(dve, batch)

        @block.gpsimd
        def _(pool):
            nc.gpsimd.memset(ident[:, :], 0.0).then_inc(ident_made, 1)
            pool.wait_ge(ident_made, 1)
            nc.gpsimd.affine_select(out=ident[:, :], in_=ident[:, :], compare_op=ALU.not_equal, fill=1.0, base=0,
                                    pattern=[[-1, P]], channel_multiplier=1).then_inc(ident_made, 1)
            nc.gpsimd.memset(causal[:, :], 0.0).then_inc(causal_made, 1)
            pool.wait_ge(causal_made, 1)
            nc.gpsimd.affine_select(out=causal[:, :], in_=causal[:, :], compare_op=ALU.is_ge, fill=MASKED,
                                    base=0, pattern=[[-1, P]], channel_multiplier=1).then_inc(causal_made, 1)
            pool.wait_ge(ident_made, 2)
            nc.gpsimd.tensor_copy(ident16[:, :], ident[:, :]).then_inc(causal_made, 1)
            pool.wait_ge(mix_in, 16 * (1 + 2 + 1 + T))
            pool.wait_ge(post_spread, 2)
            for c in range(WC):
                if c >= 2:
                    pool.wait_ge(wo_used, c - 1)
                nc.gpsimd.tensor_tensor(wo_mix[:, c % 2], wo_s[:, c, :].unsqueeze(1).to_broadcast([P, H, D]),
                                        post_x[:, c, :].unsqueeze(2).to_broadcast([P, H, D]),
                                        ALU.mult).then_inc(wo_mixed, 1)
            pool.wait_ge(a_taken, 4)
            nc.gpsimd.tensor_copy(a_now[:, :], a_all[:, 0, :]).then_inc(a_ready, 1)
            pool.wait_ge(consts_made, 3)

            def norm_scale(kind, b, what):
                n = ln_index(kind, b, what)
                pool.wait_ge(ln_meanvar, 4 * (n + 1))
                alone(pool)
                nc.gpsimd.tensor_scalar(vareps[:, :], meanvar[:, :, 1:2].squeeze(2), EPS, None, ALU.add).then_inc(ln_vareps, 1)
                pool.wait_ge(ln_vareps, n + 1)
                at_least(pool, ln_out, 4 * n)
                alone(pool)
                nc.gpsimd.tensor_tensor(rstd[:, :], vareps[:, :], minus_half[:, :], ALU.pow).then_inc(ln_rstd, 1)

            norm_scale("pro", 0, "x")
            pool.wait_ge(umem_in, 16 * H)

            def batch(kind, b):
                def step(s):
                    g = b * H + s
                    fixed = isinstance(s, int)
                    if kind != "drain":
                        pool.wait_ge(misc_full, misc_index(kind, b, ("G", s)) + 1)
                        alone(pool)
                        nxt = (s + 1) % H
                        nc.gpsimd.tensor_copy(a_now[:, :], a_all[:, bass.ds(nxt, 1), :].squeeze(1)).then_inc(a_ready, 1)
                        if fixed and s == 0:
                            pool.wait_ge(misc_free, misc_index(kind, b, ("MEM", 1)) + 1)
                        slot = ring(head_of(s, 0), RING)
                        if kind != "first" or not (fixed and s < RING):
                            pool.wait_ge(probs_ready, 4 * (g - RING + 1))
                        alone(pool)
                        nc.gpsimd.tensor_copy(mem_parts(scores[:, bass.ds(slot, 1), :].squeeze(1)),
                                              head_mem(smem, s)).then_inc(mem_placed, 1)
                    if lagged(kind, s, LAG_P):
                        gp = g - LAG_P
                        pool.wait_ge(rinv_ready, gp + 1)
                        at_least(pool, t_full, 4 * gp)
                        nc.gpsimd.tensor_tensor(diag[:, :, :], ident[:, :].unsqueeze(1).to_broadcast([P, T, P]),
                                                rinv[:, :].unsqueeze(2).to_broadcast([P, T, P]),
                                                ALU.mult).then_inc(diag_ready, 1)
                        if fixed and s == LAG_P and kind != "first":
                            pool.wait_ge(misc_full, misc_index(kind, b, ("PM", 1)) + 1)
                        alone(pool)
                        nc.gpsimd.tensor_tensor(
                            head_mem(pmem, head_of(s, LAG_P)), mem_parts(probs[:, :]),
                            rinv[:, :].rearrange("p (a t) -> p a t", a=2).unsqueeze(3).to_broadcast([P, 2, 2, M]),
                            ALU.mult).then_inc(pmem_ready, 1)
                    if lagged(kind, s, 1):
                        gn = g - 1
                        pool.wait_ge(masked, 4 * gn + 4)
                        alone(pool)
                        slot = ring(head_of(s, 1), RING)
                        nc.gpsimd.tensor_tensor(negmax[:, bass.ds(slot, 1), :].squeeze(1),
                                                rowmax[:, bass.ds(slot, 1), :].squeeze(1), minus_one[:, :],
                                                ALU.mult).then_inc(negmax_ready, 1)
                    if not fixed:
                        return
                    if s == 0 and kind in ("first", "mid"):
                        norm_scale(kind, b, "x")
                    if kind == "first":
                        return
                    if s == 5:
                        norm_scale(kind, b, "Y")
                        norm_scale(kind, b, "X1")
                    if s == 9:
                        pool.wait_ge(misc_free, misc_index(kind, b, ("UP", 2)) + 1)
                        alone(pool)
                        nc.gpsimd.tensor_scalar(f_exp[:, :, :], f_exp[:, :, :], 1.0, None, ALU.add).then_inc(silu_pool, 1)
                        nc.gpsimd.tensor_tensor(f_up[:, :, :], f_up[:, :, :], f_gate[:, :, :], ALU.mult).then_inc(silu_pool, 1)
                    if s == 11:
                        norm_scale(kind, b, "Z")

                steps(pool, kind, step)

            batches(pool, batch)


_INS = ['L0_attn_x', 'L0_attn_Wq', 'L0_attn_Wk', 'L0_attn_Wv', 'L0_attn_pre_proj', 'L0_attn_post_proj',
        'L0_attn_mem_k', 'L0_attn_mem_v', 'L0_attn_Wo', 'L0_attn_bo', 'L0_ffn_w_gate', 'L0_ffn_w_up',
        'L0_ffn_w_down']
_OUTS = [((B, N, D), 'float32')]


def kernel(**inputs):
    import numpy as _np
    import concourse.bacc as _bacc
    from concourse import mybir as _mybir
    from concourse.bass_utils import run_bass_kernel_spmd as _run

    nc = _bacc.Bacc("TRN2", target_bir_lowering=False, num_devices=1)
    arrays, args = {}, []
    for name in _INS:
        a = _np.ascontiguousarray(inputs[name])
        arrays[f"in_{name}_dram"] = a
        args.append(nc.dram_tensor(f"in_{name}_dram", a.shape, _mybir.dt.from_np(a.dtype), kind="ExternalInput").ap())
    for i, (shape, dtype) in enumerate(_OUTS):
        dt = _mybir.dt.from_np(_np.dtype(dtype))
        args.append(nc.dram_tensor(f"out_{i}_dram", shape, dt, kind="ExternalOutput").ap())
    build(nc, *args)
    r = _run(nc, [arrays], core_ids=[0])
    got = tuple(r.results[0][f"out_{i}_dram"] for i in range(len(_OUTS)))
    return got[0]
```

```python
from contextlib import ExitStack

import concourse.bass as bass
from concourse import mybir

F32 = mybir.dt.float32
BF16 = mybir.dt.bfloat16
I32 = mybir.dt.int32
ALU = mybir.AluOpType
ACT = mybir.ActivationFunctionType
AX_X = mybir.AxisListType.X

P = 128
B, N, D = 16, 512, 128
H, DH, M = 16, 64, 16
TOPK = 64
HID = 384
T = N // P
HC = HID // P
WC = H * DH // P
EPS = 1e-5
FMAX = 3.4028234663852886e38
MASKED = -2.0 ** 100

KEYS = [P * (t + 1) for t in range(T)]
ROW = [k + M for k in KEYS]
AT = [sum(ROW[:t]) for t in range(T)]
KEY_AT = [AT[t] + M * (t % 2) for t in range(T)]
WIDE = sum(ROW)
MEM_AT = KEYS[0]
ORDER = [3, 2, 1, 0]
RING = 8
ERING = 2
GUESSES = 3
LAG_K = 4
LAG_P = 5
PEEL = 12

U_STEPS = {5: (0, 4), 6: (4, 7), 7: (7, 10), 8: (10, 13), 9: (13, 16)}
FFN_STEPS = {6: [("X1T",), ("GATE", 0), ("UP", 0)], 7: [("GATE", 1), ("UP", 1)],
             8: [("GATE", 2), ("UP", 2)], 10: [("DOWN",)]}


OPENING = [("G", H), ("MEM", 0), ("MEM", 1)]

AIM = TOPK - 4
WINDOW = 4

S_T, S_LAST, S_OTHER, S_SLOPE, S_PARTS = 0, 1, 4, 7, 8


def guess_table():
    import math

    import numpy as np

    def above(z):
        return 0.5 * math.erfc(z / math.sqrt(2))

    def pdf(z):
        return math.exp(-z * z / 2) / math.sqrt(2 * math.pi)

    def quantile(share):
        low, high = -8.0, 8.0
        for _ in range(60):
            middle = (low + high) / 2
            low, high = (middle, high) if above(middle) > share else (low, middle)
        return low

    table = np.zeros((P, 2 * T + GUESSES * T + T * 9 + 2 * T), np.float32)
    for t in range(T):
        for i in range(P):
            n = P * t + i + 1
            z = quantile(min(max((AIM - 0.4 * M) / n, 0.02), 0.97))
            density = n * pdf(z) + M * pdf(z / 4.4) / 4.4
            active = n + M > TOPK
            table[i, t] = z
            table[i, T + t] = 1 / (2 * density)
            table[i, 5 * T + 9 * T + t] = float(active)
            table[i, 5 * T + 10 * T + t] = FMAX if active else -FMAX
        for k in range(GUESSES):
            table[:, 2 * T + k * T + t] = ROW[t] - 2 * AIM - 0.25
        table[:, 5 * T + 9 * t:5 * T + 9 * t + 9] = np.arange(9) - TOPK
    return table


def lagged(kind, s, lag):
    if not isinstance(s, int):
        return True
    return not (kind == "first" and s < lag) and not (kind == "drain" and s >= lag)


def flagged(kind, s):
    return lagged(kind, s, LAG_K)


def misc_order(kind):
    uses = []
    if kind == "pro":
        return [("XT",)] + [("U", u) for u in range(16)] + OPENING
    for s in range(PEEL if kind == "drain" else H):
        if kind != "drain":
            uses.append(("SQ", s))
            if s < H - 1:
                uses.append(("G", s + 1))
            elif kind != "last":
                uses += OPENING
        if s == 1 and kind in ("first", "mid"):
            uses.append(("XT",))
        if kind != "first":
            if s == 4:
                uses += [("PM", 0), ("PM", 1)]
            uses += FFN_STEPS.get(s, [])
        if kind in ("first", "mid") and s in U_STEPS:
            uses += [("U", u) for u in range(*U_STEPS[s])]
        if flagged(kind, s):
            uses.append(("FLAG", s))
    return uses


KINDS = ("pro", "first", "mid", "last", "drain")
USES = {k: misc_order(k) for k in KINDS}
PLACE = {k: {u: i for i, u in enumerate(USES[k])} for k in KINDS}


def misc_index(kind, b, use):
    n = 0 if kind == "pro" else len(USES["pro"])
    if kind in ("mid", "last", "drain"):
        n += len(USES["first"])
    if kind == "mid":
        n = (b - 1) * len(USES["mid"]) + n
    if kind in ("last", "drain"):
        n += len(USES["mid"]) * (B - 2)
    if kind == "drain":
        n += len(USES["last"])
    if not isinstance(use[1] if len(use) > 1 else 0, int):
        return n + PLACE[kind][(use[0], PEEL)] - 3 * PEEL + 3 * use[1]
    return n + PLACE[kind][use]


def opening_index(kind, b, use):
    if kind == "first":
        return misc_index("pro", 0, use)
    return misc_index(kind, b, USES[kind][0]) - len(OPENING) - 1 + OPENING.index(use)


def g_index(kind, b, s):
    if isinstance(s, int) and s == 0:
        return opening_index(kind, b, ("G", H))
    return misc_index(kind, b, ("G", s))


def flag_index(kind, b, s):
    if not isinstance(s, int) or s > 0:
        if isinstance(s, int) or kind == "drain":
            return misc_index(kind, b, ("FLAG", s - 1))
        return misc_index(kind, b, ("FLAG", s)) - 3
    return misc_index(kind, b, ("FLAG", 0)) - PLACE[kind][("FLAG", 0)] - 1


def ln_index(kind, b, what):
    at = {"x": 0, "Y": 1, "X1": 2, "Z": 3}[what]
    if kind == "pro":
        return 0
    if kind == "first":
        return 1
    if kind == "mid":
        return (b - 1) * 4 + 2 + at
    return 2 + 4 * (B - 2) + (at - 1) + (3 if kind == "drain" else 0)


def batches(engine, body):
    body("first", 0)
    with engine.Fori(1, B - 1) as b:
        body("mid", b)
    body("last", B - 1)
    body("drain", B)


def steps(engine, kind, step):
    for s in range(PEEL):
        step(s)
    if kind != "drain":
        with engine.Fori(PEEL, H - 1) as h:
            step(h)
        step(H - 1)


def head_of(s, lag):
    return (s - lag) % H if isinstance(s, int) else s - lag


def batch_of(b, s, lag):
    return b - 1 if isinstance(s, int) and s < lag else b


def at_least(engine, semaphore, value):
    if isinstance(value, int) and value <= 0:
        return
    engine.wait_ge(semaphore, value)


def alone(engine):
    engine.nop(nofuse=True)


def build(nc, table, x, wq, wk, wv, pre, post, memk, memv, wo, bo, wgate, wup, wdown, out):
    with ExitStack() as ctx:
        def sb(name, shape, dt=F32):
            return ctx.enter_context(nc.sbuf_tensor(name, shape, dt))

        def ps(name, shape):
            return ctx.enter_context(nc.psum_tensor(name, shape, F32))

        def sem(name):
            return ctx.enter_context(nc.semaphore(name))

        scores = sb("scores", [P, RING, WIDE])
        expo = sb("expo", [P, ERING, WIDE])
        work = sb("work", [P, WIDE])
        probs = sb("probs", [P, WIDE])
        probsT = sb("probsT", [P, 2, N])
        u_all = sb("u_all", [P, 2, T, H * D])
        a_all = sb("a_all", [P, H, D])
        b_all = sb("b_all", [P, H, D])
        amem = sb("amem", [P, H, M])
        umem = sb("umem", [P, 2, D])
        a_now = sb("a_now", [P, D])
        gT = sb("gT", [P, N])
        xcur = sb("xcur", [P, N])
        xnext = sb("xnext", [P, N])
        xwork = sb("xwork", [P, T, D])
        xres = sb("xres", [P, T, D])
        ybuf = sb("ybuf", [P, T, D])
        x1T = sb("x1T", [P, N])
        f_tanh = sb("f_tanh", [P, HC, N])
        f_gate = sb("f_gate", [P, HC, N])
        f_up = sb("f_up", [P, HC, N])
        wgT = sb("wgT", [P, HC, P])
        wuT = sb("wuT", [P, HC, P])
        wdT = sb("wdT", [P, HC, P])
        smem = sb("smem", [P, T, H, M])
        pmem = sb("pmem", [P, T, H, M])
        pmemT = sb("pmemT", [P, 2, N])
        causal = sb("causal", [P, P], BF16)
        ident16 = sb("ident16", [P, P], BF16)
        ident = sb("ident", [P, P])
        gsq = sb("gsq", [P, N])
        consts = sb("consts", [P, 16 * T])
        state = sb("state", [P, S_PARTS, (GUESSES + 1) * T])
        moved = sb("moved", [P, S_PARTS, GUESSES * T])
        counts = sb("counts", [P, GUESSES * T])
        part3 = sb("part3", [P, 3, GUESSES * T])
        cross = sb("cross", [P, GUESSES * T])
        slope = sb("slope", [P, GUESSES * T])
        over = sb("over", [P, GUESSES * T])
        miss2 = sb("miss2", [P, GUESSES * T])
        gnorm2 = sb("gnorm2", [P, T])
        gnorm = sb("gnorm", [P, T])
        plus_half = sb("plus_half", [P, T])
        onesP = sb("onesP", [P, 1])
        signs = sb("signs", [P, GUESSES, ROW[T - 1]], mybir.dt.int8)
        cand = sb("cand", [P, T, 9])
        found = sb("found", [P, T])
        offset = sb("offset", [P, T, 9])
        short = sb("short", [P, T])
        missed = sb("missed", [P, T])
        bad = sb("bad", [P, 1])
        flag = sb("flag", [1, 1])
        ones = sb("ones", [1, P])
        bias = sb("bias", [1, D])
        memmax = sb("memmax", [P, T, H])
        rowmax = sb("rowmax", [P, RING, T])
        negmax = sb("negmax", [P, RING, T])
        kth = sb("kth", [P, RING, T])
        top8 = sb("top8", [P, T, 8])
        rowsum = sb("rowsum", [P, T])
        rinv = sb("rinv", [P, T])
        stats = sb("stats", [P, T, 6])
        meanvar = sb("meanvar", [P, T, 2])
        vareps = sb("vareps", [P, T])
        rstd = sb("rstd", [P, T])
        minus_half = sb("minus_half", [P, T])
        minus_one = sb("minus_one", [P, GUESSES * T])

        flat_u = u_all[:, :, :, :].rearrange("p a t n -> p (a t n)")
        take = [0]

        def cut(n):
            a = flat_u[:, take[0]:take[0] + n]
            take[0] += n
            return a

        wq_s, wk_s, wv_s = cut(WC * P), cut(WC * P), cut(WC * P)
        wqT = cut(WC * P).rearrange("p (c n) -> p c n", c=WC)
        wkT = cut(WC * (P + M)).rearrange("p (c n) -> p c n", c=WC)
        wvT = cut(WC * P).rearrange("p (c n) -> p c n", c=WC)
        mvT = cut(WC * M).rearrange("p (c n) -> p c n", c=WC)
        wo_s = cut(WC * D).rearrange("p (c n) -> p c n", c=WC)
        wk_mix = cut(2 * H * (P + M)).rearrange("p (a h n) -> p a h n", a=2, h=H)
        flat_s = scores[:, :, :].rearrange("p a n -> p (a n)")
        wo_mix = flat_s[:, 0:2 * H * D].rearrange("p (a h n) -> p a h n", a=2, h=H)
        umem_flat = flat_s[:, 2 * H * D:3 * H * D]
        mem_s = flat_s[:, 3 * H * D:3 * H * D + 512].rearrange("p (a g n) -> p a g n", a=2, g=2)
        flat_e = expo[:, :, :].rearrange("p a n -> p (a n)")
        pre_x = flat_e[:, 0:P].rearrange("p (c k) -> p c k", c=WC)
        post_x = flat_e[:, P:2 * P].rearrange("p (c h) -> p c h", c=WC)
        post_raw = flat_e[:, 2 * P:4 * P]
        w_int = flat_e[:, 4 * P:4 * P + 3 * HID].bitcast(I32).rearrange("p (a c n) -> p a c n", a=3, c=HC)
        w_f = f_tanh[:, :, :].rearrange("p c n -> p (c n)")[:, 0:3 * HID].rearrange("p (a c n) -> p a c n", a=3, c=HC)

        s_bank = [ps(f"s_bank{i}", [P, N]) for i in range(4)]
        t_bank = [ps(f"t_bank{i}", [P, N]) for i in range(2)]
        y_bank = ps("y_bank", [P, N])
        misc = ps("misc", [P, N])

        w_in = sem("w_in")
        mix_in = sem("mix_in")
        x_in = sem("x_in")
        res_in = sem("res_in")
        out_sent = sem("out_sent")
        umem_in = sem("umem_in")
        ident_made = sem("ident_made")
        causal_made = sem("causal_made")
        consts_made = sem("consts_made")
        ffn_w_ready = sem("ffn_w_ready")
        turn_full = sem("turn_full")
        turn_taken = sem("turn_taken")
        post_spread = sem("post_spread")
        wk_mixed = sem("wk_mixed")
        wk_used = sem("wk_used")
        wo_mixed = sem("wo_mixed")
        wo_used = sem("wo_used")
        a_taken = sem("a_taken")
        b_taken = sem("b_taken")
        misc_full = sem("misc_full")
        misc_free = sem("misc_free")
        xcur_ready = sem("xcur_ready")
        a_ready = sem("a_ready")
        scores_full = sem("scores_full")
        masked = sem("masked")
        memmax_ready = sem("memmax_ready")
        mem_placed = sem("mem_placed")
        negmax_ready = sem("negmax_ready")
        exp_ready = sem("exp_ready")
        table_in = sem("table_in")
        gsq_ready = sem("gsq_ready")
        gnorm_step = sem("gnorm_step")
        state_set = sem("state_set")
        guess_step = sem("guess_step")
        first_ready = sem("first_ready")
        guess_ready = sem("guess_ready")
        counted = [sem(f"counted{k}") for k in range(GUESSES)]
        guess_taken = sem("guess_taken")
        select_step = sem("select_step")
        bad_ready = sem("bad_ready")
        scaled = sem("scaled")
        topk_step = sem("topk_step")
        kth_ready = sem("kth_ready")
        probs_ready = sem("probs_ready")
        rinv_ready = sem("rinv_ready")
        pmem_ready = sem("pmem_ready")
        t_full = sem("t_full")
        t_taken = sem("t_taken")
        pv_done = sem("pv_done")
        y_full = sem("y_full")
        y_taken = sem("y_taken")
        ln_stats = sem("ln_stats")
        ln_meanvar = sem("ln_meanvar")
        ln_vareps = sem("ln_vareps")
        ln_rstd = sem("ln_rstd")
        ln_out = sem("ln_out")
        x1_ready = sem("x1_ready")
        out_ready = sem("out_ready")
        silu_pool = sem("silu_pool")
        silu_ready = sem("silu_ready")

        x_t = x.rearrange("b (t p) d -> b p t d", p=P)
        out_t = out.rearrange("b (t p) d -> b p t d", p=P)
        banks = s_bank + t_bank + [y_bank, misc]

        def row(tensor, slot, t):
            return tensor[:, bass.ds(slot, 1), AT[t]:AT[t] + ROW[t]].squeeze(1)

        def keys(tensor, slot, t):
            return tensor[:, bass.ds(slot, 1), KEY_AT[t]:KEY_AT[t] + KEYS[t]].squeeze(1)

        def mem_parts(flat):
            return flat.rearrange("p (a c) -> p a c", a=2)[:, :, MEM_AT:MEM_AT + 2 * M].rearrange(
                "p a (t m) -> p a t m", t=2)

        def head_mem(tensor, h):
            return tensor[:, :, bass.ds(h, 1), :].rearrange("p (a t) h m -> p a t (h m)", a=2)

        def ring(g, size):
            return g % size

        turns = []
        for w_s in (wq_s, wk_s, wv_s):
            for half in range(2):
                turns.append([w_s[:, (4 * half + i) * P:(4 * half + i + 1) * P] for i in range(4)])
        for a in range(2):
            turns.append([mem_s[:, a, g, :] for g in range(2)])
        for a in range(3):
            turns.append([w_f[:, a, c, :] for c in range(HC)])

        first_guess, first_slope = consts[:, 0:T], consts[:, T:2 * T]
        aim_sum = consts[:, 2 * T:5 * T]
        ranks = consts[:, 5 * T:14 * T].rearrange("p (t n) -> p t n", t=T)
        active, cap = consts[:, 14 * T:15 * T], consts[:, 15 * T:16 * T]
        ALL = GUESSES * T

        block = ctx.enter_context(nc.Block())

        @block.sync
        def _(sp):
            sp.sem_inc(out_ready, 1)
            sp.sem_inc(silu_ready, 1)
            sp.sem_inc(out_sent, 16)
            sp.dma_start(consts[:, :], table).then_inc(table_in, 16)
            sp.dma_start(wq_s, wq).then_inc(w_in, 16)
            sp.dma_start(wk_s, wk).then_inc(w_in, 16)
            sp.dma_start(wv_s, wv).then_inc(w_in, 16)
            for a, mem in enumerate((memk, memv)):
                for copy in range(2):
                    sp.dma_start(mem_s[:, a, :, copy * DH:(copy + 1) * DH],
                                 mem.rearrange("(g h) m c -> (h m) g c", g=2)).then_inc(w_in, 16)
            sp.dma_start(w_int[:, 0], wgate.rearrange("(c p) d -> p c d", p=P)).then_inc(w_in, 16)
            sp.dma_start(w_int[:, 1], wup.rearrange("(c p) d -> p c d", p=P)).then_inc(w_in, 16)
            sp.dma_start(w_int[:, 2], wdown.rearrange("p (c d) -> p c d", c=HC)).then_inc(w_in, 16)
            sp.dma_start(wo_s, wo.rearrange("(c p) o -> p c o", p=P)).then_inc(mix_in, 16)
            for half in range(2):
                src = pre.rearrange("(c a) k -> a c k", a=2)[half:half + 1]
                sp.dma_start(pre_x[half * DH:(half + 1) * DH], src.to_broadcast([DH, WC, H])).then_inc(mix_in, 16)
            sp.dma_start(post_raw, post.rearrange("(a h) k -> a (h k)", a=1).to_broadcast([P, H * H])).then_inc(mix_in, 16)
            sp.dma_start(xwork[:, :, :], x_t[0]).then_inc(x_in, 16)
            sp.dma_start(bias[:, :], bo.rearrange("(a d) -> a d", a=1)).then_inc(mix_in, 16)
            sp.wait_ge(b_taken, 8)
            for h in range(H):
                sp.dma_start(umem[M * (h % 8):M * (h % 8 + 1), h // 8, :],
                             umem_flat[0:M, h * D:(h + 1) * D]).then_inc(umem_in, 16)
            sp.wait_ge(misc_full, misc_index("pro", 0, ("XT",)) + 1)
            sp.dma_start(xwork[:, :, :], x_t[1]).then_inc(x_in, 16)

            def batch(kind, b):
                if kind != "first":
                    sp.wait_ge(out_ready, b)
                    sp.dma_start(xres[:, :, :], x_t[bass.ds(b - 1, 1)].squeeze(0)).then_inc(res_in, 16)
                if kind in ("first", "mid"):
                    last_use = ("XT",) if kind == "first" else ("X1T",)
                    sp.wait_ge(misc_full, misc_index(kind, b, last_use) + 1)
                    sp.dma_start(xwork[:, :, :], x_t[bass.ds((b + 2) % B, 1)].squeeze(0)).then_inc(x_in, 16)
                if kind != "first":
                    sp.wait_ge(out_ready, b + 1)
                    sp.dma_start(out_t[bass.ds(b - 1, 1)].squeeze(0), ybuf[:, :, :]).then_inc(out_sent, 16)

            batches(sp, batch)
            sp.wait_ge(out_sent, 16 * (B + 1))

        @block.tensor
        def _(pe):
            pe.wait_ge(ident_made, 2)
            pe.wait_ge(causal_made, 3)
            pe.wait_ge(w_in, 16 * 10)
            pe.wait_ge(consts_made, 5)
            for i, group in enumerate(turns):
                if i >= 8:
                    pe.wait_ge(turn_taken, i - 7)
                if i == 8:
                    pe.wait_ge(ffn_w_ready, 3)
                for j, src in enumerate(group):
                    mm = nc.tensor.transpose(banks[i % 8][:, j * P:(j + 1) * P], src, ident[:, :])
                mm.then_inc(turn_full, 1)
            pe.wait_ge(turn_taken, len(turns))
            for c in range(WC):
                pe.wait_ge(wk_mixed, c + 1)
                for q in range(4):
                    nc.tensor.matmul(banks[q][:, :], lhsT=wqT[:, c, :], rhs=wk_mix[:, c % 2, 4 * q:4 * q + 4, 0:P],
                                     start=(c == 0), stop=(c == WC - 1))
                nc.tensor.matmul(banks[4][:, 0:H * M], lhsT=wqT[:, c, :], rhs=wk_mix[:, c % 2, :, P:P + M],
                                 start=(c == 0), stop=(c == WC - 1)).then_inc(wk_used, 1)
            pe.wait_ge(a_taken, 5)
            for c in range(WC):
                pe.wait_ge(wo_mixed, c + 1)
                for q in range(4):
                    rhs = wo_mix[:, c % 2, 4 * q:4 * q + 4, :]
                    nc.tensor.matmul(banks[q][:, :], lhsT=wvT[:, c, :], rhs=rhs, start=(c == 0), stop=(c == WC - 1))
                    mm = nc.tensor.matmul(banks[4 + q][0:M, :], lhsT=mvT[:, c, :], rhs=rhs,
                                          start=(c == 0), stop=(c == WC - 1))
                mm.then_inc(wo_used, 1)
            pe.wait_ge(b_taken, 8)
            pe.wait_ge(umem_in, 16 * H)

            def share(kind, b, use):
                at_least(pe, misc_free, misc_index(kind, b, use))

            def turn_x(kind, b):
                pe.wait_ge(ln_out, 4 * (ln_index(kind, b, "x") + 1))
                share(kind, b, ("XT",))
                for t in range(T):
                    mm = nc.tensor.transpose(misc[:, t * P:(t + 1) * P], xwork[:, t, :], ident[:, :])
                mm.then_inc(misc_full, 1)

            def values(kind, b, u):
                share(kind, b, ("U", u))
                nc.tensor.matmul(misc[:, :], lhsT=xnext[:, (u // 4) * P:(u // 4 + 1) * P],
                                 rhs=b_all[:, 4 * (u % 4):4 * (u % 4) + 4, :], start=True, stop=True).then_inc(misc_full, 1)

            def start_y():
                nc.tensor.matmul(y_bank[:, :], lhsT=ones[:, :], rhs=bias[:, :].unsqueeze(1).to_broadcast([1, T, D]), start=True, stop=False,
                                 skip_group_check=True)

            turn_x("pro", 0)
            for u in range(16):
                values("pro", 0, u)
            start_y()

            def product_g(kind, b, s, count):
                pe.wait_ge(a_ready, count)
                share(kind, b, ("G", s))
                nc.tensor.matmul(misc[:, :], lhsT=a_now[:, :], rhs=xcur[:, :], start=True,
                                 stop=True).then_inc(misc_full, 1)

            def open_batch(kind, b, batches_done):
                pe.wait_ge(xcur_ready, batches_done + 1)
                product_g(kind, b, H, H * batches_done + 1)
                for j in range(2):
                    share(kind, b, ("MEM", j))
                    for i in range(2):
                        t = 2 * j + i
                        mm = nc.tensor.matmul(misc[:, i * H * M:(i + 1) * H * M],
                                              lhsT=xcur[:, t * P:(t + 1) * P], rhs=amem[:, :, :],
                                              start=True, stop=True)
                    mm.then_inc(misc_full, 1)

            open_batch("pro", 0, 0)

            def post(kind, b, s, g):
                h, par = head_of(s, LAG_P), batch_of(b, s, LAG_P) % 2
                def pv(p):
                    t, n = ORDER[p], 4 * g + p
                    pe.wait_ge(t_taken, n + 1)
                    for j in range(t + 1):
                        mm = nc.tensor.matmul(
                            y_bank[:, t * P:(t + 1) * P], lhsT=probsT[:, p % 2, j * P:(j + 1) * P],
                            rhs=u_all[:, bass.ds(par, 1), j, bass.ds(h * D, D)].squeeze(1),
                            start=False, stop=False, skip_group_check=True)
                    mm.then_inc(pv_done, 1)

                for p, t in enumerate(ORDER):
                    n = 4 * g + p
                    pe.wait_ge(scaled, n + 1)
                    at_least(pe, t_taken, n - 1)
                    for j in range(t + 1):
                        mm = nc.tensor.transpose(t_bank[p % 2][:, j * P:(j + 1) * P],
                                                 probs[:, KEY_AT[t] + j * P:KEY_AT[t] + (j + 1) * P], ident[:, :])
                    mm.then_inc(t_full, 1)
                    if p >= 1:
                        pv(p - 1)
                pv(3)

            def batch(kind, b):
                def step(s):
                    g = b * H + s
                    if kind != "drain":
                        pe.wait_ge(gsq_ready, g + 1)
                        share(kind, b, ("SQ", s))
                        for t in range(T):
                            mm = nc.tensor.matmul(misc[:, t:t + 1], lhsT=gsq[:, t * P:(t + 1) * P], rhs=onesP[:, :],
                                                  start=True, stop=True)
                        mm.then_inc(misc_full, 1)
                        pe.wait_ge(misc_free, g_index(kind, b, s) + 1)
                        for p, t in enumerate(ORDER):
                            n = 4 * g + p
                            at_least(pe, masked, n - 3)
                            nc.tensor.matmul(s_bank[p][:, 0:KEYS[t]], lhsT=gT[:, t * P:(t + 1) * P],
                                             rhs=xcur[:, 0:KEYS[t]], start=True, stop=False, skip_group_check=True)
                            nc.tensor.matmul(s_bank[p][:, t * P:(t + 1) * P], lhsT=ident16[:, :], rhs=causal[:, :],
                                             start=False, stop=True, skip_group_check=True).then_inc(scores_full, 1)
                        if not (isinstance(s, int) and s == H - 1):
                            product_g(kind, b, s + 1, g + 2)
                        elif kind != "last":
                            open_batch(kind, b, b + 1)
                    if lagged(kind, s, LAG_P):
                        post(kind, b, s, g - LAG_P)
                    if isinstance(s, int):
                        extras(kind, b, s)
                    if flagged(kind, s):
                        pe.wait_ge(bad_ready, g - LAG_K + 1)
                        share(kind, b, ("FLAG", s))
                        nc.tensor.matmul(misc[0:1, 0:1], lhsT=bad[:, :], rhs=onesP[:, :], start=True,
                                         stop=True).then_inc(misc_full, 1)

                def extras(kind, b, s):
                    if s == 1 and kind in ("first", "mid"):
                        turn_x(kind, b)
                    if kind != "first" and s == 4:
                        pe.wait_ge(pmem_ready, b * H)
                        for j in range(2):
                            share(kind, b, ("PM", j))
                            for i in range(2):
                                for half in range(2):
                                    k = 2 * i + half
                                    mm = nc.tensor.transpose(misc[:, k * P:(k + 1) * P],
                                                             pmem[:, 2 * j + i, 8 * half:8 * half + 8, :], ident[:, :])
                            mm.then_inc(misc_full, 1)
                        pe.wait_ge(misc_free, misc_index(kind, b, ("PM", 1)) + 1)
                        for t in range(T):
                            for half in range(2):
                                k = 2 * (t % 2) + half
                                mm = nc.tensor.matmul(y_bank[:, t * P:(t + 1) * P],
                                                      lhsT=pmemT[:, t // 2, k * P:(k + 1) * P], rhs=umem[:, half, :],
                                                      start=False, stop=True, skip_group_check=True)
                        mm.then_inc(y_full, 1)
                        if kind != "drain":
                            pe.wait_ge(y_taken, b)
                            start_y()
                    if kind != "first":
                        for use in FFN_STEPS.get(s, []):
                            if use[0] == "X1T":
                                pe.wait_ge(ln_out, 4 * (ln_index(kind, b, "X1") + 1))
                            if use[0] == "DOWN":
                                pe.wait_ge(silu_ready, b + 1)
                            share(kind, b, use)
                            if use[0] == "X1T":
                                for t in range(T):
                                    mm = nc.tensor.transpose(misc[:, t * P:(t + 1) * P], xwork[:, t, :], ident[:, :])
                            elif use[0] == "DOWN":
                                for t in range(T):
                                    for c in range(HC):
                                        mm = nc.tensor.matmul(misc[:, t * P:(t + 1) * P],
                                                              lhsT=f_up[:, c, t * P:(t + 1) * P], rhs=wdT[:, c, :],
                                                              start=(c == 0), stop=(c == HC - 1))
                            else:
                                w = wgT if use[0] == "GATE" else wuT
                                mm = nc.tensor.matmul(misc[:, :], lhsT=w[:, use[1], :], rhs=x1T[:, :],
                                                      start=True, stop=True)
                            mm.then_inc(misc_full, 1)
                    if kind in ("first", "mid") and s in U_STEPS:
                        for u in range(*U_STEPS[s]):
                            values(kind, b, u)

                steps(pe, kind, step)

            batches(pe, batch)

        @block.scalar
        def _(act):
            taken = []
            for i, wT in enumerate((wqT, wkT, wvT)):
                for half in range(2):
                    taken.append([(wT[:, 4 * half:4 * half + 4, 0:P], None)])
            for i, mT in enumerate((wkT[:, :, P:P + M], mvT)):
                taken.append([(mT, i)])
            for wT in (wgT, wuT, wdT):
                taken.append([(wT[:, :, :], None)])
            for i, ((dst, mem),) in enumerate(taken):
                act.wait_ge(turn_full, i + 1)
                if mem is None:
                    n = dst.shape[1]
                    nc.scalar.copy(dst, banks[i % 8][:, 0:n * P].rearrange("p (c n) -> p c n", c=n)).then_inc(turn_taken, 1)
                else:
                    src = banks[i % 8][:, 0:H * M].rearrange("p (c a m) -> p c a m", a=2, m=M)
                    nc.scalar.copy(dst[0:DH], src[0:DH, :, 0, :])
                    nc.scalar.copy(dst[DH:P], src[DH:P, :, 1, :]).then_inc(turn_taken, 1)
            act.wait_ge(wk_used, WC)
            for q in range(4):
                nc.scalar.mul(a_all[:, 4 * q:4 * q + 4, :], banks[q][:, :].rearrange("p (h n) -> p h n", h=4),
                              DH ** -0.5).then_inc(a_taken, 1)
            nc.scalar.mul(amem[:, :, :], banks[4][:, 0:H * M].rearrange("p (h n) -> p h n", h=H),
                          DH ** -0.5).then_inc(a_taken, 1)
            act.wait_ge(wo_used, WC)
            for q in range(4):
                nc.scalar.copy(b_all[:, 4 * q:4 * q + 4, :],
                               banks[q][:, :].rearrange("p (h n) -> p h n", h=4)).then_inc(b_taken, 1)
            for q in range(4):
                nc.scalar.copy(umem_flat[0:M, q * 512:(q + 1) * 512], banks[4 + q][0:M, :]).then_inc(b_taken, 1)

            def take(kind, b, use, dst, src=None):
                act.wait_ge(misc_full, misc_index(kind, b, use) + 1)
                nc.scalar.copy(dst, misc[:, :] if src is None else src).then_inc(misc_free, 1)

            def take_values(kind, b, u, par):
                dst = u_all[:, bass.ds(par, 1), u // 4, 512 * (u % 4):512 * (u % 4 + 1)].squeeze(1)
                take(kind, b, ("U", u), dst)

            take("pro", 0, ("XT",), xnext[:, :])
            act.wait_ge(umem_in, 16 * H)
            for u in range(16):
                take_values("pro", 0, u, 0)

            def take_opening(kind, b, batches_done):
                act.wait_ge(misc_free, misc_index(kind, b, ("XT",)) + 1)
                at_least(act, scores_full, 4 * H * batches_done)
                nc.scalar.copy(xcur[:, :], xnext[:, :]).then_inc(xcur_ready, 1)
                at_least(act, gsq_ready, H * batches_done)
                take(kind, b, ("G", H), gT[:, :])
                at_least(act, mem_placed, H * batches_done)
                at_least(act, memmax_ready, batches_done)
                for j in range(2):
                    take(kind, b, ("MEM", j), smem[:, 2 * j:2 * j + 2, :, :],
                         misc[:, :].rearrange("p (t h m) -> p t h m", t=2, h=H))

            take_opening("pro", 0, 0)

            def batch(kind, b):
                def step(s):
                    g = b * H + s
                    fixed = isinstance(s, int)

                    def count(k):
                        if not lagged(kind, s, k + 1):
                            return
                        at_least(act, first_ready if k == 0 else guess_ready, g if k == 0 else g - 1)
                        act.wait_ge(masked, 4 * (g - k))
                        act.wait_ge(mem_placed, g - k)
                        for p, t in enumerate(ORDER):
                            at_least(act, counted[k], 4 * (g - k - 1) + p)
                            nc.scalar.activation(signs[:, k, 0:ROW[t]], row(scores, ring(head_of(s, k + 1), RING), t),
                                                 ACT.Sign, bias=state[:, S_T, k * T + t:k * T + t + 1], scale=-1.0,
                                                 accum_out=counts[:, k * T + t:k * T + t + 1]
                                                 ).then_inc(counted[k], 1)

                    def take_turned(p):
                        if lagged(kind, s, LAG_P):
                            n, t = 4 * (g - LAG_P) + p, ORDER[p]
                            act.wait_ge(t_full, n + 1)
                            at_least(act, pv_done, n - 1)
                            nc.scalar.copy(probsT[:, p % 2, 0:KEYS[t]], t_bank[p % 2][:, 0:KEYS[t]]).then_inc(t_taken, 1)

                    def exponentials(p):
                        if lagged(kind, s, LAG_K):
                            ge, t = g - LAG_K, ORDER[p]
                            if p == 0:
                                act.wait_ge(negmax_ready, ge + 1)
                                at_least(act, probs_ready, 4 * (ge - 1))
                            nc.scalar.activation(row(expo, ring(head_of(s, LAG_K), ERING), t),
                                                 row(scores, ring(head_of(s, LAG_K), RING), t), ACT.Exp,
                                                 bias=negmax[:, bass.ds(ring(head_of(s, LAG_K), RING), 1), t]
                                                 ).then_inc(exp_ready, 1)

                    count(2)
                    if kind != "drain":
                        take(kind, b, ("SQ", s), gnorm2[:, :], misc[:, 0:T])
                    count(1)
                    count(0)
                    if kind != "drain" and not (fixed and s == H - 1):
                        act.wait_ge(scores_full, 4 * (g + 1))
                        act.wait_ge(gsq_ready, g + 1)
                        take(kind, b, ("G", s + 1), gT[:, :])
                    elif kind in ("first", "mid"):
                        take_opening(kind, b, b + 1)
                    take_turned(0)
                    exponentials(0)
                    take_turned(1)
                    exponentials(1)
                    take_turned(2)
                    exponentials(2)
                    take_turned(3)
                    exponentials(3)
                    if fixed:
                        extras(kind, b, s)
                    if flagged(kind, s):
                        at_least(act, probs_ready, 4 * (g - LAG_K))
                        take(kind, b, ("FLAG", s), flag[:, :], misc[0:1, 0:1])

                def extras(kind, b, s):
                    if s == 1 and kind in ("first", "mid"):
                        take(kind, b, ("XT",), xnext[:, :])
                    if kind != "first" and s == 4:
                        for j in range(2):
                            take(kind, b, ("PM", j), pmemT[:, j, :])
                        act.wait_ge(y_full, b)
                        act.wait_ge(out_sent, 16 * b)
                        nc.scalar.copy(ybuf[:, :, :], y_bank[:, :].rearrange("p (t d) -> p t d", t=T)).then_inc(y_taken, 1)
                    if kind != "first":
                        for use in FFN_STEPS.get(s, []):
                            if use[0] == "X1T":
                                take(kind, b, use, x1T[:, :])
                            elif use[0] == "GATE":
                                act.wait_ge(silu_ready, b)
                                act.wait_ge(misc_full, misc_index(kind, b, use) + 1)
                                nc.scalar.activation(f_tanh[:, use[1], :], misc[:, :], ACT.Tanh, scale=0.5)
                                nc.scalar.copy(f_gate[:, use[1], :], misc[:, :]).then_inc(misc_free, 1)
                            elif use[0] == "UP":
                                take(kind, b, use, f_up[:, use[1], :])
                            else:
                                act.wait_ge(misc_full, misc_index(kind, b, use) + 1)
                                nc.scalar.mul(ybuf[:, :, :], misc[:, :].rearrange("p (t d) -> p t d", t=T),
                                              0.5).then_inc(misc_free, 1)
                    if kind in ("first", "mid") and s in U_STEPS:
                        for u in range(*U_STEPS[s]):
                            take_values(kind, b, u, (b + 1) % 2)

                steps(act, kind, step)

            batches(act, batch)

        @block.vector
        def _(dve):
            nc.vector.memset(minus_half[:, :], -0.5).then_inc(consts_made, 1)
            nc.vector.memset(plus_half[:, :], 0.5).then_inc(consts_made, 1)
            nc.vector.memset(onesP[:, :], 1.0).then_inc(consts_made, 1)
            nc.vector.memset(minus_one[:, :], -1.0).then_inc(consts_made, 1)
            nc.vector.memset(ones[:, :], 1.0).then_inc(consts_made, 1)
            dve.wait_ge(mix_in, 16 * 5)
            for a in range(2):
                nc.vector.tensor_copy(post_x[a * DH:(a + 1) * DH], post_raw[a * DH:(a + 1) * DH].rearrange(
                    "p (h c a) -> p a c h", a=2, c=WC)[:, a]).then_inc(post_spread, 1)
            dve.wait_ge(w_in, 16 * 10)
            for a in range(3):
                nc.vector.tensor_scalar(w_f[:, a], w_int[:, a], 1.0 / 127.0, None, ALU.mult).then_inc(ffn_w_ready, 1)
            dve.wait_ge(turn_taken, 8)
            for c in range(WC):
                if c >= 2:
                    dve.wait_ge(wk_used, c - 1)
                nc.vector.tensor_tensor(wk_mix[:, c % 2], wkT[:, c, :].unsqueeze(1).to_broadcast([P, H, P + M]),
                                        pre_x[:, c, :].unsqueeze(2).to_broadcast([P, H, P + M]),
                                        ALU.mult).then_inc(wk_mixed, 1)

            def norm_stats(kind, b, what, src):
                n = ln_index(kind, b, what)
                for t in range(T):
                    nc.vector.bn_stats(stats[:, t, :], src[:, t, :]).then_inc(ln_stats, 1)
                dve.wait_ge(ln_stats, 4 * (n + 1))
                alone(dve)
                for t in range(T):
                    nc.vector.bn_aggr(meanvar[:, t, :], stats[:, t, :]).then_inc(ln_meanvar, 1)

            def norm_apply(kind, b, what, dst, src):
                n = ln_index(kind, b, what)
                dve.wait_ge(ln_rstd, n + 1)
                for t in range(T):
                    nc.vector.tensor_scalar(dst[:, t, :], src[:, t, :], meanvar[:, t, 0:1], rstd[:, t:t + 1],
                                            ALU.subtract, ALU.mult).then_inc(ln_out, 1)

            dve.wait_ge(x_in, 16)
            norm_stats("pro", 0, "x", xwork)
            norm_apply("pro", 0, "x", xwork, xwork)

            def general_kth(slot):
                for t in ORDER:
                    nc.vector.tensor_copy(work[:, AT[t]:AT[t] + ROW[t]], row(scores, slot, t)).then_inc(topk_step, 1)
                for i in range(15):
                    for p, t in enumerate(ORDER):
                        wrk = work[:, AT[t]:AT[t] + ROW[t]]
                        dve.wait_ge(topk_step, T * i + p + 1)
                        if i % 2 == 0:
                            nc.vector.max(cand[:, t, 0:8], wrk).then_inc(topk_step, 1)
                        else:
                            nc.vector.match_replace(wrk, cand[:, t, 0:8], wrk, -FMAX).then_inc(topk_step, 1)
                dve.wait_ge(topk_step, 16 * T)
                nc.vector.tensor_copy(kth[:, bass.ds(slot, 1), :].squeeze(1),
                                      cand[:, :, 7:8].squeeze(2)).then_inc(topk_step, 1)
                dve.wait_ge(topk_step, 16 * T + 1)
                dve.sem_clear(topk_step)

            dve.wait_ge(table_in, 16)
            dve.wait_ge(state_set, 5)

            def move_guesses():
                v = nc.vector
                guess, first = state[:, S_T, 0:ALL], state[:, S_SLOPE, 0:ALL]
                miss, last = moved[:, S_LAST + 1, :], state[:, S_LAST + 1, 0:ALL]
                three_last = state[:, S_LAST:S_LAST + 3, 0:ALL]
                three_other = state[:, S_OTHER:S_OTHER + 3, 0:ALL]
                v.tensor_tensor(miss, counts[:, :], aim_sum, ALU.subtract).then_inc(guess_step, 1)
                v.tensor_tensor(part3[:, :, :], three_last, three_other, ALU.subtract).then_inc(guess_step, 1)
                v.tensor_copy(moved[:, S_LAST, :], guess).then_inc(guess_step, 1)
                v.tensor_copy(moved[:, S_SLOPE, :], first).then_inc(guess_step, 1)
                dve.wait_ge(guess_step, 1)
                v.tensor_tensor(cross[:, :], miss, last, ALU.mult).then_inc(guess_step, 1)
                v.tensor_tensor(miss2[:, :], miss, miss, ALU.mult).then_inc(guess_step, 1)
                dve.wait_ge(guess_step, 5)
                v.scalar_tensor_tensor(out=part3[:, :, :], in0=cross[:, :].unsqueeze(1).to_broadcast([P, 3, ALL]),
                                       scalar=0.0, in1=part3[:, :, :], op0=ALU.is_lt,
                                       op1=ALU.mult).then_inc(guess_step, 1)
                dve.wait_ge(guess_step, 6)
                v.scalar_tensor_tensor(out=miss2[:, :], in0=miss2[:, :], scalar=(2 * WINDOW + 0.25) ** 2 + 1.0,
                                       in1=miss, op0=ALU.is_gt, op1=ALU.mult).then_inc(guess_step, 1)
                dve.wait_ge(guess_step, 7)
                v.tensor_tensor(moved[:, S_OTHER:S_OTHER + 3, :], three_other, part3[:, :, :],
                                ALU.add).then_inc(guess_step, 1)
                dve.wait_ge(guess_step, 9)
                v.tensor_tensor(over[:, :], miss, moved[:, S_OTHER + 1, :], ALU.subtract).then_inc(guess_step, 1)
                v.tensor_tensor(slope[:, :], guess, moved[:, S_OTHER, :], ALU.subtract).then_inc(guess_step, 1)
                dve.wait_ge(guess_step, 10)
                v.reciprocal(over[:, :], over[:, :]).then_inc(guess_step, 1)
                dve.wait_ge(guess_step, 12)
                v.tensor_tensor(slope[:, :], slope[:, :], over[:, :], ALU.mult).then_inc(guess_step, 1)
                dve.wait_ge(guess_step, 13)
                v.tensor_tensor(slope[:, :], slope[:, :], first, ALU.subtract).then_inc(guess_step, 1)
                dve.wait_ge(guess_step, 14)
                v.tensor_tensor(slope[:, :], slope[:, :], moved[:, S_OTHER + 2, :], ALU.mult).then_inc(guess_step, 1)
                dve.wait_ge(guess_step, 15)
                v.tensor_tensor(slope[:, :], slope[:, :], first, ALU.add).then_inc(guess_step, 1)
                dve.wait_ge(guess_step, 16)
                v.tensor_tensor(slope[:, :], slope[:, :], miss2[:, :], ALU.mult).then_inc(guess_step, 1)
                dve.wait_ge(guess_step, 17)
                v.tensor_tensor(moved[:, S_T, :], guess, slope[:, :], ALU.subtract).then_inc(guess_step, 1)
                dve.wait_ge(guess_step, 18)
                dve.sem_clear(guess_step)
                v.tensor_copy(state[:, :, T:T + ALL], moved[:, :, :]).then_inc(guess_ready, 1)

            def batch(kind, b):
                def step(s):
                    g = b * H + s
                    fixed = isinstance(s, int)
                    if fixed and s == 0 and kind in ("first", "mid"):
                        dve.wait_ge(x_in, 16 * (b + 2))
                        norm_stats(kind, b, "x", xwork)
                    if fixed and s == 5 and kind != "first":
                        dve.wait_ge(y_taken, b)
                        norm_stats(kind, b, "Y", ybuf)
                    if fixed and s == 6 and kind != "first":
                        if kind != "drain" and kind != "last":
                            dve.wait_ge(misc_full, misc_index(kind, b, ("XT",)) + 1)
                        norm_apply(kind, b, "X1", xwork, xres)
                    if fixed and s == 11 and kind != "first":
                        dve.wait_ge(misc_free, misc_index(kind, b, ("DOWN",)) + 1)
                        norm_stats(kind, b, "Z", ybuf)
                    if lagged(kind, s, LAG_P):
                        gp = g - LAG_P
                        slot = ring(head_of(s, LAG_P), RING)
                        dve.wait_ge(exp_ready, 4 * gp + 4)
                        at_least(dve, t_full, 4 * gp)
                        at_least(dve, pmem_ready, gp)
                        at_least(dve, scaled, 4 * gp)
                        dve.wait_ge(kth_ready, gp + 1)
                        dve.wait_ge(misc_free, flag_index(kind, b, s) + 1)
                        alone(dve)
                        rows_missed = dve.value_load(flag[0:1, 0:1].bitcast(I32), min_val=0, max_val=2 ** 31 - 1)
                        with dve.If(rows_missed > 0):
                            general_kth(slot)
                        for t in ORDER:
                            nc.vector.scalar_tensor_tensor(
                                out=probs[:, AT[t]:AT[t] + ROW[t]], in0=row(scores, slot, t),
                                scalar=kth[:, bass.ds(slot, 1), t], in1=row(expo, ring(head_of(s, LAG_P), ERING), t),
                                op0=ALU.is_ge, op1=ALU.mult, accum_out=rowsum[:, t:t + 1]).then_inc(probs_ready, 1)
                        dve.wait_ge(probs_ready, 4 * gp + 4)
                        nc.vector.reciprocal(rinv[:, :], rowsum[:, :]).then_inc(rinv_ready, 1)
                    if lagged(kind, s, LAG_K):
                        gk = g - LAG_K
                        dve.wait_ge(mem_placed, gk + 1)
                        dve.wait_ge(masked, 4 * gk + 4)
                        slot = ring(head_of(s, LAG_K), RING)
                        dve.wait_ge(guess_ready, g - 1)
                        nc.vector.tensor_copy(cand[:, :, 0:1].squeeze(2),
                                              state[:, S_T, GUESSES * T:(GUESSES + 1) * T]).then_inc(guess_taken, 1)
                        dve.wait_ge(guess_taken, gk + 1)
                        for t in ORDER:
                            nc.vector.tensor_scalar(work[:, AT[t]:AT[t] + ROW[t]], row(scores, slot, t),
                                                    cand[:, t, 0:1], None, ALU.is_ge, ALU.add,
                                                    accum_out=found[:, t:t + 1]).then_inc(select_step, 1)
                        for p, t in enumerate(ORDER):
                            wrk = work[:, AT[t]:AT[t] + ROW[t]]
                            dve.wait_ge(select_step, p + 1)
                            nc.vector.scalar_tensor_tensor(out=wrk, in0=wrk, scalar=-FMAX, in1=row(scores, slot, t),
                                                           op0=ALU.mult, op1=ALU.add).then_inc(select_step, 1)
                        for p, t in enumerate(ORDER):
                            dve.wait_ge(select_step, T + p + 1)
                            nc.vector.max(cand[:, t, 1:9], work[:, AT[t]:AT[t] + ROW[t]]).then_inc(select_step, 1)
                        nc.vector.tensor_tensor(offset[:, :, :], ranks, found[:, :].unsqueeze(2).to_broadcast([P, T, 9]),
                                                ALU.add).then_inc(select_step, 1)
                        nc.vector.tensor_scalar(short[:, :], found[:, :], -float(AIM), None, ALU.add).then_inc(select_step, 1)
                        dve.wait_ge(select_step, 3 * T + 2)
                        nc.vector.scalar_tensor_tensor(out=offset[:, :, :], in0=offset[:, :, :], scalar=0.0,
                                                       in1=cand[:, :, :], op0=ALU.is_equal,
                                                       op1=ALU.mult).then_inc(select_step, 1)
                        nc.vector.tensor_tensor(missed[:, :], short[:, :], short[:, :], ALU.mult).then_inc(select_step, 1)
                        dve.wait_ge(select_step, 3 * T + 4)
                        nc.vector.tensor_reduce(short[:, :], offset[:, :, :], AX_X, ALU.add).then_inc(select_step, 1)
                        at_least(dve, misc_full, flag_index(kind, b, s) + 1 if lagged(kind, s, LAG_P) else 0)
                        nc.vector.scalar_tensor_tensor(out=missed[:, :], in0=missed[:, :], scalar=WINDOW ** 2 + 0.5,
                                                       in1=active, op0=ALU.is_gt, op1=ALU.mult,
                                                       accum_out=bad[:, :]).then_inc(bad_ready, 1)
                        dve.wait_ge(select_step, 3 * T + 5)
                        dve.sem_clear(select_step)
                        nc.vector.tensor_tensor(kth[:, bass.ds(slot, 1), :].squeeze(1), short[:, :], cap,
                                                ALU.min).then_inc(kth_ready, 1)
                    if any(lagged(kind, s, k + 1) for k in range(GUESSES)):
                        for k in range(GUESSES):
                            if lagged(kind, s, k + 1):
                                dve.wait_ge(counted[k], 4 * (g - k))
                        at_least(dve, first_ready, g if lagged(kind, s, 1) else 0)
                        alone(dve)
                        move_guesses()
                    if fixed and s == 0 and kind != "drain":
                        dve.wait_ge(misc_free, opening_index(kind, b, ("MEM", 1)) + 1)
                        nc.vector.reduce_max(memmax[:, :, :].rearrange("p t h -> p (t h)"),
                                             smem[:, :, :, :].rearrange("p t h m -> p (t h) m"),
                                             AX_X).then_inc(memmax_ready, 1)
                    if kind != "drain":
                        if fixed and s == 0:
                            dve.wait_ge(memmax_ready, b + 1)
                        slot = ring(head_of(s, 0), RING)
                        for p, t in enumerate(ORDER):
                            dve.wait_ge(scores_full, 4 * g + p + 1)
                            nc.vector.tensor_scalar(keys(scores, slot, t), s_bank[p][:, 0:KEYS[t]], 1.0,
                                                    memmax[:, t, bass.ds(s, 1)], ALU.mult, ALU.max,
                                                    accum_out=rowmax[:, bass.ds(slot, 1), t]).then_inc(masked, 1)
                    if not fixed:
                        return
                    if s == 0 and kind in ("first", "mid"):
                        norm_apply(kind, b, "x", xwork, xwork)
                    if kind == "first":
                        return
                    if s == 5:
                        norm_apply(kind, b, "Y", ybuf, ybuf)
                        dve.wait_ge(res_in, 16 * b)
                        dve.wait_ge(ln_out, 4 * (ln_index(kind, b, "Y") + 1))
                        nc.vector.tensor_tensor(xres[:, :, :], xres[:, :, :], ybuf[:, :, :], ALU.add).then_inc(x1_ready, 1)
                        dve.wait_ge(x1_ready, b)
                        norm_stats(kind, b, "X1", xres)
                    if s == 9:
                        dve.wait_ge(silu_pool, b)
                        nc.vector.scalar_tensor_tensor(out=f_up[:, :, :], in0=f_tanh[:, :, :], scalar=1.0,
                                                       in1=f_up[:, :, :], op0=ALU.add, op1=ALU.mult).then_inc(silu_ready, 1)
                    if s == 11:
                        norm_apply(kind, b, "Z", ybuf, ybuf)
                        dve.wait_ge(ln_out, 4 * (ln_index(kind, b, "Z") + 1))
                        nc.vector.tensor_tensor(ybuf[:, :, :], xres[:, :, :], ybuf[:, :, :], ALU.add).then_inc(out_ready, 1)

                steps(dve, kind, step)

            batches(dve, batch)

        @block.gpsimd
        def _(pool):
            nc.gpsimd.memset(ident[:, :], 0.0).then_inc(ident_made, 1)
            pool.wait_ge(ident_made, 1)
            nc.gpsimd.affine_select(out=ident[:, :], in_=ident[:, :], compare_op=ALU.not_equal, fill=1.0, base=0,
                                    pattern=[[-1, P]], channel_multiplier=1).then_inc(ident_made, 1)
            nc.gpsimd.memset(causal[:, :], 0.0).then_inc(causal_made, 1)
            pool.wait_ge(causal_made, 1)
            nc.gpsimd.affine_select(out=causal[:, :], in_=causal[:, :], compare_op=ALU.is_ge, fill=MASKED,
                                    base=0, pattern=[[-1, P]], channel_multiplier=1).then_inc(causal_made, 1)
            pool.wait_ge(ident_made, 2)
            nc.gpsimd.tensor_copy(ident16[:, :], ident[:, :]).then_inc(causal_made, 1)
            pool.wait_ge(mix_in, 16 * 5)
            pool.wait_ge(post_spread, 2)
            for c in range(WC):
                if c >= 2:
                    pool.wait_ge(wo_used, c - 1)
                nc.gpsimd.tensor_tensor(wo_mix[:, c % 2], wo_s[:, c, :].unsqueeze(1).to_broadcast([P, H, D]),
                                        post_x[:, c, :].unsqueeze(2).to_broadcast([P, H, D]),
                                        ALU.mult).then_inc(wo_mixed, 1)
            pool.wait_ge(a_taken, 4)
            nc.gpsimd.tensor_copy(a_now[:, :], a_all[:, 0, :]).then_inc(a_ready, 1)
            pool.wait_ge(consts_made, 5)

            def norm_scale(kind, b, what):
                n = ln_index(kind, b, what)
                pool.wait_ge(ln_meanvar, 4 * (n + 1))
                alone(pool)
                nc.gpsimd.tensor_scalar(vareps[:, :], meanvar[:, :, 1:2].squeeze(2), EPS, None, ALU.add).then_inc(ln_vareps, 1)
                pool.wait_ge(ln_vareps, n + 1)
                at_least(pool, ln_out, 4 * n)
                alone(pool)
                nc.gpsimd.tensor_tensor(rstd[:, :], vareps[:, :], minus_half[:, :], ALU.pow).then_inc(ln_rstd, 1)

            norm_scale("pro", 0, "x")
            pool.wait_ge(umem_in, 16 * H)
            nc.gpsimd.memset(state[:, :, :], 0.0).then_inc(state_set, 1)
            nc.gpsimd.memset(moved[:, :, :], 0.0).then_inc(state_set, 1)
            nc.gpsimd.memset(counts[:, :], 0.0).then_inc(state_set, 1)
            pool.wait_ge(state_set, 3)
            nc.gpsimd.memset(state[:, S_LAST + 2, :], 1.0).then_inc(state_set, 1)
            nc.gpsimd.memset(moved[:, S_LAST + 2, :], 1.0).then_inc(state_set, 1)
            pool.wait_ge(state_set, 5)
            pool.wait_ge(table_in, 16)

            def next_a(kind, b, made, after):
                pool.wait_ge(misc_full, misc_index(kind, b, ("G", made)) + 1)
                alone(pool)
                nc.gpsimd.tensor_copy(a_now[:, :], a_all[:, bass.ds(after % H, 1), :].squeeze(1)).then_inc(a_ready, 1)

            def squares(kind, b, made):
                pool.wait_ge(misc_free, misc_index(kind, b, ("G", made)) + 1)
                alone(pool)
                nc.gpsimd.tensor_tensor(gsq[:, :], gT[:, :], gT[:, :], ALU.mult).then_inc(gsq_ready, 1)

            next_a("pro", 0, H, 1)
            squares("pro", 0, H)

            def batch(kind, b):
                def step(s):
                    g = b * H + s
                    fixed = isinstance(s, int)
                    if lagged(kind, s, 1):
                        gn = g - 1
                        pool.wait_ge(masked, 4 * gn + 4)
                        alone(pool)
                        slot = ring(head_of(s, 1), RING)
                        nc.gpsimd.tensor_tensor(negmax[:, bass.ds(slot, 1), :].squeeze(1),
                                                rowmax[:, bass.ds(slot, 1), :].squeeze(1), minus_one[:, 0:T],
                                                ALU.mult).then_inc(negmax_ready, 1)
                    if kind != "drain":
                        if fixed and s == 0:
                            pool.wait_ge(misc_free, opening_index(kind, b, ("MEM", 1)) + 1)
                        slot = ring(head_of(s, 0), RING)
                        if kind != "first" or not (fixed and s < RING):
                            pool.wait_ge(probs_ready, 4 * (g - RING + 1))
                        alone(pool)
                        nc.gpsimd.tensor_copy(mem_parts(scores[:, bass.ds(slot, 1), :].squeeze(1)),
                                              head_mem(smem, s)).then_inc(mem_placed, 1)
                        pool.wait_ge(misc_free, misc_index(kind, b, ("SQ", s)) + 1)
                        at_least(pool, first_ready, g)
                        alone(pool)
                        nc.gpsimd.tensor_tensor(gnorm[:, :], gnorm2[:, :], plus_half[:, :], ALU.pow).then_inc(gnorm_step, 1)
                    if lagged(kind, s, LAG_P):
                        gp = g - LAG_P
                        pool.wait_ge(rinv_ready, gp + 1)
                        at_least(pool, probs_ready, 4 * gp + 4)
                        alone(pool)
                        for t in ORDER:
                            prb = probs[:, AT[t]:AT[t] + ROW[t]]
                            nc.gpsimd.tensor_scalar(prb, prb, rinv[:, t:t + 1], 1.0, ALU.mult,
                                                    ALU.mult).then_inc(scaled, 1)
                        if fixed and s == LAG_P and kind != "first":
                            pool.wait_ge(misc_full, misc_index(kind, b, ("PM", 1)) + 1)
                        pool.wait_ge(scaled, 4 * gp + 4)
                        alone(pool)
                        nc.gpsimd.tensor_copy(head_mem(pmem, head_of(s, LAG_P)), mem_parts(probs[:, :])).then_inc(pmem_ready, 1)
                    if kind != "drain" and not (kind == "last" and fixed and s == H - 1):
                        next_a(kind, b, s + 1, s + 2)
                        squares(kind, b, s + 1)
                    if fixed:
                        extras(kind, b, s)
                    if kind != "drain":
                        pool.wait_ge(gnorm_step, 1)
                        at_least(pool, guess_ready, g)
                        alone(pool)
                        nc.gpsimd.tensor_tensor(state[:, S_SLOPE, 0:T], gnorm[:, :], first_slope, ALU.mult).then_inc(gnorm_step, 1)
                        pool.wait_ge(gnorm_step, 2)
                        pool.sem_clear(gnorm_step)
                        nc.gpsimd.tensor_tensor(state[:, S_T, 0:T], gnorm[:, :], first_guess, ALU.mult).then_inc(first_ready, 1)

                def extras(kind, b, s):
                    if s == 0 and kind in ("first", "mid"):
                        norm_scale(kind, b, "x")
                    if kind == "first":
                        return
                    if s == 5:
                        norm_scale(kind, b, "Y")
                        norm_scale(kind, b, "X1")
                    if s == 9:
                        pool.wait_ge(misc_free, misc_index(kind, b, ("UP", 2)) + 1)
                        alone(pool)
                        nc.gpsimd.tensor_tensor(f_up[:, :, :], f_up[:, :, :], f_gate[:, :, :], ALU.mult).then_inc(silu_pool, 1)
                    if s == 11:
                        norm_scale(kind, b, "Z")

                steps(pool, kind, step)

            batches(pool, batch)


_INS = ['L0_attn_x', 'L0_attn_Wq', 'L0_attn_Wk', 'L0_attn_Wv', 'L0_attn_pre_proj', 'L0_attn_post_proj',
        'L0_attn_mem_k', 'L0_attn_mem_v', 'L0_attn_Wo', 'L0_attn_bo', 'L0_ffn_w_gate', 'L0_ffn_w_up',
        'L0_ffn_w_down']
_OUTS = [((B, N, D), 'float32')]


def kernel(**inputs):
    import numpy as _np
    import concourse.bacc as _bacc
    from concourse import mybir as _mybir
    from concourse.bass_utils import run_bass_kernel_spmd as _run

    nc = _bacc.Bacc("TRN2", target_bir_lowering=False, num_devices=1)
    arrays, args = {}, []
    table = guess_table()
    arrays["in_guess_table_dram"] = table
    args.append(nc.dram_tensor("in_guess_table_dram", table.shape, F32, kind="ExternalInput").ap())
    for name in _INS:
        a = _np.ascontiguousarray(inputs[name])
        arrays[f"in_{name}_dram"] = a
        args.append(nc.dram_tensor(f"in_{name}_dram", a.shape, _mybir.dt.from_np(a.dtype), kind="ExternalInput").ap())
    for i, (shape, dtype) in enumerate(_OUTS):
        dt = _mybir.dt.from_np(_np.dtype(dtype))
        args.append(nc.dram_tensor(f"out_{i}_dram", shape, dt, kind="ExternalOutput").ap())
    build(nc, *args)
    r = _run(nc, [arrays], core_ids=[0])
    got = tuple(r.results[0][f"out_{i}_dram"] for i in range(len(_OUTS)))
    return got[0]
```

```python
from contextlib import ExitStack

import concourse.bass as bass
from concourse import mybir

F32 = mybir.dt.float32
BF16 = mybir.dt.bfloat16
I32 = mybir.dt.int32
ALU = mybir.AluOpType
ACT = mybir.ActivationFunctionType
AX_X = mybir.AxisListType.X

P = 128
B, N, D = 16, 512, 128
H, DH, M = 16, 64, 16
TOPK = 64
HID = 384
T = N // P
HC = HID // P
WC = H * DH // P
EPS = 1e-5
FMAX = 3.4028234663852886e38
MASKED = -2.0 ** 100

KEYS = [P * (t + 1) for t in range(T)]
ROW = [k + M for k in KEYS]
AT = [sum(ROW[:t]) for t in range(T)]
KEY_AT = [AT[t] + M * (t % 2) for t in range(T)]
WIDE = sum(ROW)
MEM_AT = KEYS[0]
ORDER = [3, 2, 1, 0]
RING = 8
ERING = 2
GUESSES = 3
LAG_K = 4
LAG_P = 5

EXTRAS = {0: [("MEM", 0), ("MEM", 1), None],
          2: [None, ("XT",), None],
          3: [("U", 0), ("U", 1), None],
          4: [("U", 4), ("PM", 0), ("PM", 1)],
          5: [("U", 5), ("U", 2), None],
          6: [("U", 3), ("U", 6), ("U", 15)],
          7: [("U", 7), ("U", 8), None],
          8: [("U", 9), ("U", 10), None],
          9: [("U", 11), ("X1T",), None],
          10: [("GATE", 0), ("UP", 0), None],
          11: [("GATE", 1), ("UP", 1), None],
          12: [("GATE", 2), ("UP", 2), None],
          13: [("U", 12), ("U", 13), None],
          14: [("U", 14), ("DOWN",), None],
          15: [None, ("G", H), None]}

AIM = TOPK - 4
WINDOW = 4

S_T, S_LAST, S_OTHER, S_PARTS = 0, 1, 3, 5
FAR = 16384.0


def guess_table():
    import math

    import numpy as np

    def above(z):
        return 0.5 * math.erfc(z / math.sqrt(2))

    def pdf(z):
        return math.exp(-z * z / 2) / math.sqrt(2 * math.pi)

    def quantile(share):
        low, high = -8.0, 8.0
        for _ in range(60):
            middle = (low + high) / 2
            low, high = (middle, high) if above(middle) > share else (low, middle)
        return low

    table = np.zeros((P, 2 * T + GUESSES * T + T * 9 + 2 * T), np.float32)
    for t in range(T):
        for i in range(P):
            n = P * t + i + 1
            z = quantile(min(max((AIM - 0.4 * M) / n, 0.02), 0.97))
            density = n * pdf(z) + M * pdf(z / 4.4) / 4.4
            active = n + M > TOPK
            table[i, t] = z
            table[i, T + t] = z - FAR / (2 * density)
            table[i, 5 * T + 9 * T + t] = float(active)
            table[i, 5 * T + 10 * T + t] = FMAX if active else -FMAX
        for k in range(GUESSES):
            table[:, 2 * T + k * T + t] = ROW[t] - 2 * AIM - 0.25
        table[:, 5 * T + 9 * t:5 * T + 9 * t + 9] = np.arange(9) - TOPK
    return table


def lagged(kind, s, lag):
    return not (kind == "first" and s < lag) and not (kind == "drain" and s >= lag)


def flagged(kind, s):
    return lagged(kind, s, LAG_K)


def extra(kind, s, place):
    use = EXTRAS.get(s, [None] * 3)[place]
    if use is None:
        return None
    if use[0] == "MEM":
        wanted = ("first", "mid", "last")
    elif use[0] in ("XT", "U", "G"):
        wanted = ("first", "mid")
    else:
        wanted = ("mid", "last", "drain")
    return use if kind in wanted else None


def misc_order(kind):
    if kind == "pro":
        return [("XT",), ("G", H)]
    uses = []
    for s in range(H):
        if kind != "drain":
            uses.append(("SQ", s))
        uses.append(extra(kind, s, 0))
        if kind != "drain" and s < H - 1:
            uses.append(("G", s + 1))
        uses.append(extra(kind, s, 1))
        if flagged(kind, s):
            uses.append(("FLAG", s))
        uses.append(extra(kind, s, 2))
    return [use for use in uses if use is not None]


KINDS = ("pro", "first", "mid", "last", "drain")
USES = {k: misc_order(k) for k in KINDS}
PLACE = {k: {u: i for i, u in enumerate(USES[k])} for k in KINDS}


def misc_index(kind, b, use):
    n = 0 if kind == "pro" else len(USES["pro"])
    if kind in ("mid", "last", "drain"):
        n += len(USES["first"])
    if kind == "mid":
        n = (b - 1) * len(USES["mid"]) + n
    if kind in ("last", "drain"):
        n += len(USES["mid"]) * (B - 2)
    if kind == "drain":
        n += len(USES["last"])
    return n + PLACE[kind][use]


def g_index(kind, b, s):
    if s > 0:
        return misc_index(kind, b, ("G", s))
    if kind == "first":
        return misc_index("pro", 0, ("G", H))
    return misc_index(kind, b, USES[kind][0]) - 2


def flag_index(kind, b, s):
    if s > 0:
        return misc_index(kind, b, ("FLAG", s - 1))
    return misc_index(kind, b, USES[kind][0]) - 1


def ln_index(kind, b, what):
    at = {"x": 0, "Y": 1, "X1": 2, "Z": 3}[what]
    if kind == "pro":
        return 0
    if kind == "first":
        return 1
    if kind == "mid":
        return (b - 1) * 4 + 2 + at
    return 2 + 4 * (B - 2) + (at - 1) + (3 if kind == "drain" else 0)


def batches(engine, body):
    body("first", 0)
    with engine.Fori(1, B - 1) as b:
        body("mid", b)
    body("last", B - 1)
    body("drain", B)


def head_of(s, lag):
    return (s - lag) % H


def batch_of(b, s, lag):
    return b - 1 if s < lag else b


def at_least(engine, semaphore, value):
    if isinstance(value, int) and value <= 0:
        return
    engine.wait_ge(semaphore, value)


def alone(engine):
    engine.nop(nofuse=True)


def build(nc, table, x, wq, wk, wv, pre, post, memk, memv, wo, bo, wgate, wup, wdown, out):
    with ExitStack() as ctx:
        def sb(name, shape, dt=F32):
            return ctx.enter_context(nc.sbuf_tensor(name, shape, dt))

        def ps(name, shape):
            return ctx.enter_context(nc.psum_tensor(name, shape, F32))

        def sem(name):
            return ctx.enter_context(nc.semaphore(name))

        scores = sb("scores", [P, RING, WIDE])
        expo = sb("expo", [P, ERING, WIDE])
        work = sb("work", [P, WIDE])
        probs = sb("probs", [P, WIDE])
        probsT = sb("probsT", [P, 2, N])
        u_all = sb("u_all", [P, 2, T, H * D])
        a_all = sb("a_all", [P, H, D])
        b_all = sb("b_all", [P, H, D])
        amem = sb("amem", [P, H, M])
        umem = sb("umem", [P, 2, D])
        a_now = sb("a_now", [P, D])
        gT = sb("gT", [P, N])
        xcur = sb("xcur", [P, N])
        xnext = sb("xnext", [P, N])
        xwork = sb("xwork", [P, T, D])
        xres = sb("xres", [P, T, D])
        ybuf = sb("ybuf", [P, T, D])
        x1T = sb("x1T", [P, N])
        f_tanh = sb("f_tanh", [P, HC, N])
        f_gate = sb("f_gate", [P, HC, N])
        f_up = sb("f_up", [P, HC, N])
        wgT = sb("wgT", [P, HC, P])
        wuT = sb("wuT", [P, HC, P])
        wdT = sb("wdT", [P, HC, P])
        smem = sb("smem", [P, T, H, M])
        pmem = sb("pmem", [P, T, H, M])
        pmemT = sb("pmemT", [P, 2, N])
        causal = sb("causal", [P, P], BF16)
        ident16 = sb("ident16", [P, P], BF16)
        ident = sb("ident", [P, P])
        gsq = sb("gsq", [P, N])
        consts = sb("consts", [P, 16 * T])
        state = sb("state", [P, 2, S_PARTS, (GUESSES + 1) * T])
        counts = sb("counts", [P, GUESSES * T])
        between = sb("between", [P, 2, GUESSES * T])
        cross = sb("cross", [P, GUESSES * T])
        move = sb("move", [P, GUESSES * T])
        over = sb("over", [P, GUESSES * T])
        miss2 = sb("miss2", [P, GUESSES * T])
        gnorm2 = sb("gnorm2", [P, T])
        gnorm = sb("gnorm", [P, T])
        plus_half = sb("plus_half", [P, T])
        onesP = sb("onesP", [P, 1])
        signs = sb("signs", [P, GUESSES, ROW[T - 1]], mybir.dt.int8)
        cand = sb("cand", [P, T, 9])
        found = sb("found", [P, T])
        offset = sb("offset", [P, T, 9])
        short = sb("short", [P, T])
        off_aim = sb("off_aim", [P, T])
        missed = sb("missed", [P, T + 1])
        flags = sb("flags", [1, T + 1])
        ones = sb("ones", [1, P])
        bias = sb("bias", [1, D])
        memmax = sb("memmax", [P, T, H])
        rowmax = sb("rowmax", [P, RING, T])
        negmax = sb("negmax", [P, RING, T])
        kth = sb("kth", [P, RING, T])
        top8 = sb("top8", [P, 8])
        rowsum = sb("rowsum", [P, T])
        rinv = sb("rinv", [P, T])
        stats = sb("stats", [P, T, 6])
        meanvar = sb("meanvar", [P, T, 2])
        vareps = sb("vareps", [P, T])
        rstd = sb("rstd", [P, T])
        minus_half = sb("minus_half", [P, T])
        minus_one = sb("minus_one", [P, T])

        flat_u = u_all[:, :, :, :].rearrange("p a t n -> p (a t n)")
        take = [0]

        def cut(n):
            a = flat_u[:, take[0]:take[0] + n]
            take[0] += n
            return a

        wq_s, wk_s, wv_s = cut(WC * P), cut(WC * P), cut(WC * P)
        wqT = cut(WC * P).rearrange("p (c n) -> p c n", c=WC)
        wkT = cut(WC * (P + M)).rearrange("p (c n) -> p c n", c=WC)
        wvT = cut(WC * P).rearrange("p (c n) -> p c n", c=WC)
        mvT = cut(WC * M).rearrange("p (c n) -> p c n", c=WC)
        wo_s = cut(WC * D).rearrange("p (c n) -> p c n", c=WC)
        wk_mix = cut(2 * H * (P + M)).rearrange("p (a h n) -> p a h n", a=2, h=H)
        flat_s = scores[:, :, :].rearrange("p a n -> p (a n)")
        wo_mix = flat_s[:, 0:2 * H * D].rearrange("p (a h n) -> p a h n", a=2, h=H)
        mv_mix = flat_s[:, 2 * H * D:2 * H * D + WC * H * M].rearrange("p (c h m) -> p c h m", c=WC, h=H)
        mem_s = flat_s[:, 3 * H * D:3 * H * D + 512].rearrange("p (a g n) -> p a g n", a=2, g=2)
        flat_e = expo[:, :, :].rearrange("p a n -> p (a n)")
        pre_x = flat_e[:, 0:P].rearrange("p (c k) -> p c k", c=WC)
        post_x = flat_e[:, P:2 * P].rearrange("p (c h) -> p c h", c=WC)
        post_raw = flat_e[:, 2 * P:4 * P]
        w_int = flat_e[:, 4 * P:4 * P + 3 * HID].bitcast(I32).rearrange("p (a c n) -> p a c n", a=3, c=HC)
        w_f = f_tanh[:, :, :].rearrange("p c n -> p (c n)")[:, 0:3 * HID].rearrange("p (a c n) -> p a c n", a=3, c=HC)

        s_bank = [ps(f"s_bank{i}", [P, N]) for i in range(4)]
        t_bank = [ps(f"t_bank{i}", [P, N]) for i in range(2)]
        y_bank = ps("y_bank", [P, N])
        misc = ps("misc", [P, N])

        w_in = sem("w_in")
        mix_in = sem("mix_in")
        x_in = sem("x_in")
        res_in = sem("res_in")
        out_sent = sem("out_sent")
        mv_mixed = sem("mv_mixed")
        umem_made = sem("umem_made")
        u_made = sem("u_made")
        u_taken = sem("u_taken")
        ident_made = sem("ident_made")
        causal_made = sem("causal_made")
        consts_made = sem("consts_made")
        ffn_w_ready = sem("ffn_w_ready")
        turn_full = sem("turn_full")
        turn_taken = sem("turn_taken")
        post_spread = sem("post_spread")
        wk_mixed = sem("wk_mixed")
        wk_used = sem("wk_used")
        wo_mixed = sem("wo_mixed")
        wo_used = sem("wo_used")
        a_taken = sem("a_taken")
        b_taken = sem("b_taken")
        misc_full = sem("misc_full")
        misc_free = sem("misc_free")
        xcur_ready = sem("xcur_ready")
        a_ready = sem("a_ready")
        scores_full = sem("scores_full")
        masked = sem("masked")
        memmax_ready = sem("memmax_ready")
        mem_placed = sem("mem_placed")
        negmax_ready = sem("negmax_ready")
        exp_ready = sem("exp_ready")
        table_in = sem("table_in")
        gsq_ready = sem("gsq_ready")
        gnorm_step = sem("gnorm_step")
        state_set = sem("state_set")
        guess_step = sem("guess_step")
        first_ready = sem("first_ready")
        guess_ready = sem("guess_ready")
        counted = [sem(f"counted{k}") for k in range(GUESSES)]
        guess_taken = sem("guess_taken")
        select_step = sem("select_step")
        bad_ready = sem("bad_ready")
        scaled = sem("scaled")
        topk_step = sem("topk_step")
        kth_ready = sem("kth_ready")
        probs_ready = sem("probs_ready")
        rinv_ready = sem("rinv_ready")
        pmem_ready = sem("pmem_ready")
        t_full = sem("t_full")
        t_taken = sem("t_taken")
        pv_done = sem("pv_done")
        y_full = sem("y_full")
        y_taken = sem("y_taken")
        ln_stats = sem("ln_stats")
        ln_meanvar = sem("ln_meanvar")
        ln_vareps = sem("ln_vareps")
        ln_rstd = sem("ln_rstd")
        ln_centred = sem("ln_centred")
        ln_out = sem("ln_out")
        x1_ready = sem("x1_ready")
        out_ready = sem("out_ready")
        silu_pool = sem("silu_pool")
        silu_ready = sem("silu_ready")

        x_t = x.rearrange("b (t p) d -> b p t d", p=P)
        out_t = out.rearrange("b (t p) d -> b p t d", p=P)
        banks = s_bank + t_bank + [y_bank, misc]

        def row(tensor, slot, t):
            return tensor[:, bass.ds(slot, 1), AT[t]:AT[t] + ROW[t]].squeeze(1)

        def keys(tensor, slot, t):
            return tensor[:, bass.ds(slot, 1), KEY_AT[t]:KEY_AT[t] + KEYS[t]].squeeze(1)

        def mem_parts(flat):
            return flat.rearrange("p (a c) -> p a c", a=2)[:, :, MEM_AT:MEM_AT + 2 * M].rearrange(
                "p a (t m) -> p a t m", t=2)

        def head_mem(tensor, h):
            return tensor[:, :, bass.ds(h, 1), :].rearrange("p (a t) h m -> p a t (h m)", a=2)

        def ring(g, size):
            return g % size

        turns = []
        for w_s in (wq_s, wk_s, wv_s):
            for half in range(2):
                turns.append([w_s[:, (4 * half + i) * P:(4 * half + i + 1) * P] for i in range(4)])
        for a in range(2):
            turns.append([mem_s[:, a, g, :] for g in range(2)])
        for a in range(3):
            turns.append([w_f[:, a, c, :] for c in range(HC)])

        first_guess, far_point = consts[:, 0:T], consts[:, T:2 * T]
        aim_sum = consts[:, 2 * T:5 * T]
        ranks = consts[:, 5 * T:14 * T].rearrange("p (t n) -> p t n", t=T)
        active, cap = consts[:, 14 * T:15 * T], consts[:, 15 * T:16 * T]
        ALL = GUESSES * T

        block = ctx.enter_context(nc.Block())

        @block.sync
        def _(sp):
            sp.sem_inc(out_ready, 1)
            sp.sem_inc(silu_ready, 1)
            sp.sem_inc(out_sent, 16)
            sp.dma_start(consts[:, :], table).then_inc(table_in, 16)
            sp.dma_start(wq_s, wq).then_inc(w_in, 16)
            sp.dma_start(wk_s, wk).then_inc(w_in, 16)
            sp.dma_start(wv_s, wv).then_inc(w_in, 16)
            for a, mem in enumerate((memk, memv)):
                for copy in range(2):
                    sp.dma_start(mem_s[:, a, :, copy * DH:(copy + 1) * DH],
                                 mem.rearrange("(g h) m c -> (h m) g c", g=2)).then_inc(w_in, 16)
            sp.dma_start(w_int[:, 0], wgate.rearrange("(c p) d -> p c d", p=P)).then_inc(w_in, 16)
            sp.dma_start(w_int[:, 1], wup.rearrange("(c p) d -> p c d", p=P)).then_inc(w_in, 16)
            sp.dma_start(w_int[:, 2], wdown.rearrange("p (c d) -> p c d", c=HC)).then_inc(w_in, 16)
            sp.dma_start(wo_s, wo.rearrange("(c p) o -> p c o", p=P)).then_inc(mix_in, 16)
            for half in range(2):
                src = pre.rearrange("(c a) k -> a c k", a=2)[half:half + 1]
                sp.dma_start(pre_x[half * DH:(half + 1) * DH], src.to_broadcast([DH, WC, H])).then_inc(mix_in, 16)
            sp.dma_start(post_raw, post.rearrange("(a h) k -> a (h k)", a=1).to_broadcast([P, H * H])).then_inc(mix_in, 16)
            sp.dma_start(xwork[:, :, :], x_t[0]).then_inc(x_in, 16)
            sp.dma_start(bias[:, :], bo.rearrange("(a d) -> a d", a=1)).then_inc(mix_in, 16)
            sp.wait_ge(misc_full, misc_index("pro", 0, ("XT",)) + 1)
            sp.dma_start(xwork[:, :, :], x_t[1]).then_inc(x_in, 16)

            def batch(kind, b):
                if kind != "first":
                    sp.wait_ge(out_ready, b)
                    sp.dma_start(xres[:, :, :], x_t[bass.ds(b - 1, 1)].squeeze(0)).then_inc(res_in, 16)
                if kind in ("first", "mid"):
                    last_use = ("XT",) if kind == "first" else ("X1T",)
                    sp.wait_ge(misc_full, misc_index(kind, b, last_use) + 1)
                    sp.dma_start(xwork[:, :, :], x_t[bass.ds((b + 2) % B, 1)].squeeze(0)).then_inc(x_in, 16)
                if kind != "first":
                    sp.wait_ge(out_ready, b + 1)
                    sp.dma_start(out_t[bass.ds(b - 1, 1)].squeeze(0), ybuf[:, :, :]).then_inc(out_sent, 16)

            batches(sp, batch)
            sp.wait_ge(out_sent, 16 * (B + 1))

        @block.tensor
        def _(pe):
            pe.wait_ge(ident_made, 2)
            pe.wait_ge(causal_made, 3)
            pe.wait_ge(w_in, 16 * 10)
            pe.wait_ge(consts_made, 5)
            for i, group in enumerate(turns):
                if i >= 8:
                    pe.wait_ge(turn_taken, i - 7)
                if i == 8:
                    pe.wait_ge(ffn_w_ready, 3)
                for j, src in enumerate(group):
                    mm = nc.tensor.transpose(banks[i % 8][:, j * P:(j + 1) * P], src, ident[:, :])
                mm.then_inc(turn_full, 1)
            pe.wait_ge(turn_taken, len(turns))
            for c in range(WC):
                pe.wait_ge(wk_mixed, c + 1)
                for q in range(4):
                    nc.tensor.matmul(banks[q][:, :], lhsT=wqT[:, c, :], rhs=wk_mix[:, c % 2, 4 * q:4 * q + 4, 0:P],
                                     start=(c == 0), stop=(c == WC - 1))
                nc.tensor.matmul(banks[4][:, 0:H * M], lhsT=wqT[:, c, :], rhs=wk_mix[:, c % 2, :, P:P + M],
                                 start=(c == 0), stop=(c == WC - 1)).then_inc(wk_used, 1)
            def share(kind, b, use):
                at_least(pe, misc_free, misc_index(kind, b, use))

            def turn_x(kind, b):
                pe.wait_ge(ln_out, ln_index(kind, b, "x") + 1)
                share(kind, b, ("XT",))
                for t in range(T):
                    mm = nc.tensor.transpose(misc[:, t * P:(t + 1) * P], xwork[:, t, :], ident[:, :])
                mm.then_inc(misc_full, 1)

            def values(kind, b, u):
                share(kind, b, ("U", u))
                nc.tensor.matmul(misc[:, :], lhsT=xnext[:, (u // 4) * P:(u // 4 + 1) * P],
                                 rhs=b_all[:, 4 * (u % 4):4 * (u % 4) + 4, :], start=True, stop=True).then_inc(misc_full, 1)

            def start_y():
                nc.tensor.matmul(y_bank[:, :], lhsT=ones[:, :], rhs=bias[:, :].unsqueeze(1).to_broadcast([1, T, D]), start=True, stop=False,
                                 skip_group_check=True)

            turn_x("pro", 0)
            pe.wait_ge(a_taken, 5)
            for c in range(WC):
                pe.wait_ge(wo_mixed, c + 1)
                for q in range(4):
                    mm = nc.tensor.matmul(banks[q][:, :], lhsT=wvT[:, c, :], rhs=wo_mix[:, c % 2, 4 * q:4 * q + 4, :],
                                          start=(c == 0), stop=(c == WC - 1))
                mm.then_inc(wo_used, 1)
            pe.wait_ge(mv_mixed, 1)
            for half in range(2):
                for c in range(WC):
                    mm = nc.tensor.matmul(banks[4 + half][:, 0:D], lhsT=mv_mix[:, c, 8 * half:8 * half + 8, :],
                                          rhs=wo_s[:, c, :], start=(c == 0), stop=(c == WC - 1))
                mm.then_inc(umem_made, 1)
            start_y()
            pe.wait_ge(b_taken, 6)
            pe.wait_ge(xcur_ready, 1)
            for u in range(16):
                if u >= 6:
                    pe.wait_ge(u_taken, u - 5)
                nc.tensor.matmul(banks[u % 6][:, :], lhsT=xnext[:, (u // 4) * P:(u // 4 + 1) * P],
                                 rhs=b_all[:, 4 * (u % 4):4 * (u % 4) + 4, :], start=True, stop=True).then_inc(u_made, 1)
            pe.wait_ge(u_taken, 16)

            def product_g(kind, b, s, count):
                pe.wait_ge(a_ready, count)
                share(kind, b, ("G", s))
                nc.tensor.matmul(misc[:, :], lhsT=a_now[:, :], rhs=xcur[:, :], start=True,
                                 stop=True).then_inc(misc_full, 1)

            pe.wait_ge(xcur_ready, 1)
            product_g("pro", 0, H, 1)

            def score_memory(kind, b, half):
                share(kind, b, ("MEM", half))
                for i in range(2):
                    t = 2 * half + i
                    mm = nc.tensor.matmul(misc[:, i * H * M:(i + 1) * H * M],
                                          lhsT=xcur[:, t * P:(t + 1) * P], rhs=amem[:, :, :],
                                          start=True, stop=True)
                mm.then_inc(misc_full, 1)

            def make_extra(kind, b, s, place):
                use = extra(kind, s, place)
                if use is None:
                    return
                if use[0] == "XT":
                    turn_x(kind, b)
                    return
                if use[0] == "U":
                    values(kind, b, use[1])
                    return
                if use[0] == "G":
                    pe.wait_ge(xcur_ready, b + 2)
                    product_g(kind, b, H, H * (b + 1) + 1)
                    return
                if use[0] == "MEM":
                    score_memory(kind, b, use[1])
                    return
                if use == ("PM", 0):
                    pe.wait_ge(pmem_ready, b * H)
                if use[0] == "X1T":
                    pe.wait_ge(ln_out, ln_index(kind, b, "X1") + 1)
                if use[0] == "DOWN":
                    pe.wait_ge(silu_ready, HC * b + 1)
                share(kind, b, use)
                if use[0] == "PM":
                    for i in range(2):
                        for half in range(2):
                            k = 2 * i + half
                            mm = nc.tensor.transpose(misc[:, k * P:(k + 1) * P],
                                                     pmem[:, 2 * use[1] + i, 8 * half:8 * half + 8, :], ident[:, :])
                elif use[0] == "X1T":
                    for t in range(T):
                        mm = nc.tensor.transpose(misc[:, t * P:(t + 1) * P], xwork[:, t, :], ident[:, :])
                elif use[0] == "DOWN":
                    for t in range(T):
                        for c in range(HC):
                            mm = nc.tensor.matmul(misc[:, t * P:(t + 1) * P],
                                                  lhsT=f_up[:, c, t * P:(t + 1) * P], rhs=wdT[:, c, :],
                                                  start=(c == 0), stop=(c == HC - 1))
                else:
                    w = wgT if use[0] == "GATE" else wuT
                    mm = nc.tensor.matmul(misc[:, :], lhsT=w[:, use[1], :], rhs=x1T[:, :], start=True, stop=True)
                mm.then_inc(misc_full, 1)

            def memory_y(kind, b):
                pe.wait_ge(misc_free, misc_index(kind, b, ("PM", 1)) + 1)
                for t in range(T):
                    for half in range(2):
                        k = 2 * (t % 2) + half
                        mm = nc.tensor.matmul(y_bank[:, t * P:(t + 1) * P],
                                              lhsT=pmemT[:, t // 2, k * P:(k + 1) * P], rhs=umem[:, half, :],
                                              start=False, stop=True, skip_group_check=True)
                mm.then_inc(y_full, 1)

            def post(kind, b, s, g):
                h, par = head_of(s, LAG_P), batch_of(b, s, LAG_P) % 2

                def turn(p):
                    t, n = ORDER[p], 4 * g + p
                    pe.wait_ge(scaled, n + 1)
                    at_least(pe, t_taken, n - 1)
                    for j in range(t + 1):
                        mm = nc.tensor.transpose(t_bank[p % 2][:, j * P:(j + 1) * P],
                                                 probs[:, KEY_AT[t] + j * P:KEY_AT[t] + (j + 1) * P], ident[:, :])
                    mm.then_inc(t_full, 1)

                def pv(p):
                    t, n = ORDER[p], 4 * g + p
                    pe.wait_ge(t_taken, n + 1)
                    for j in range(t + 1):
                        mm = nc.tensor.matmul(
                            y_bank[:, t * P:(t + 1) * P], lhsT=probsT[:, p % 2, j * P:(j + 1) * P],
                            rhs=u_all[:, bass.ds(par, 1), j, bass.ds(h * D, D)].squeeze(1),
                            start=False, stop=False, skip_group_check=True)
                    mm.then_inc(pv_done, 1)

                if lagged(kind, s, LAG_P):
                    turn(0)
                    turn(1)
                make_extra(kind, b, s, 1)
                if lagged(kind, s, LAG_P):
                    pv(0)
                    turn(2)
                if flagged(kind, s):
                    pe.wait_ge(bad_ready, g + LAG_P - LAG_K + 1)
                    share(kind, b, ("FLAG", s))
                    nc.tensor.matmul(misc[0:1, 0:T + 1], lhsT=onesP[:, :], rhs=missed[:, :], start=True,
                                     stop=True).then_inc(misc_full, 1)
                if lagged(kind, s, LAG_P):
                    pv(1)
                    turn(3)
                make_extra(kind, b, s, 2)
                if lagged(kind, s, LAG_P):
                    pv(2)
                    pv(3)

            def batch(kind, b):
                def step(s):
                    g = b * H + s
                    if kind != "drain":
                        pe.wait_ge(gsq_ready, g + 1)
                        share(kind, b, ("SQ", s))
                        for t in range(T):
                            mm = nc.tensor.matmul(misc[:, t:t + 1], lhsT=gsq[:, t * P:(t + 1) * P], rhs=onesP[:, :],
                                                  start=True, stop=True)
                        mm.then_inc(misc_full, 1)
                        pe.wait_ge(misc_free, g_index(kind, b, s) + 1)
                        for p, t in enumerate(ORDER):
                            n = 4 * g + p
                            at_least(pe, masked, n - 3)
                            nc.tensor.matmul(s_bank[p][:, 0:KEYS[t]], lhsT=gT[:, t * P:(t + 1) * P],
                                             rhs=xcur[:, 0:KEYS[t]], start=True, stop=False, skip_group_check=True)
                            nc.tensor.matmul(s_bank[p][:, t * P:(t + 1) * P], lhsT=ident16[:, :], rhs=causal[:, :],
                                             start=False, stop=True, skip_group_check=True).then_inc(scores_full, 1)
                            if p == 1:
                                make_extra(kind, b, s, 0)
                        if s < H - 1:
                            product_g(kind, b, s + 1, g + 2)
                    else:
                        make_extra(kind, b, s, 0)
                    if s == LAG_P and kind in ("mid", "last"):
                        pe.wait_ge(y_taken, b)
                        start_y()
                    post(kind, b, s, g - LAG_P)
                    if s == LAG_P - 1 and kind != "first":
                        memory_y(kind, b)

                for s in range(H):
                    step(s)

            batches(pe, batch)

        @block.scalar
        def _(act):
            taken = []
            for i, wT in enumerate((wqT, wkT, wvT)):
                for half in range(2):
                    taken.append([(wT[:, 4 * half:4 * half + 4, 0:P], None)])
            for i, mT in enumerate((wkT[:, :, P:P + M], mvT)):
                taken.append([(mT, i)])
            for wT in (wgT, wuT, wdT):
                taken.append([(wT[:, :, :], None)])
            for i, ((dst, mem),) in enumerate(taken):
                act.wait_ge(turn_full, i + 1)
                if mem is None:
                    n = dst.shape[1]
                    nc.scalar.copy(dst, banks[i % 8][:, 0:n * P].rearrange("p (c n) -> p c n", c=n)).then_inc(turn_taken, 1)
                else:
                    src = banks[i % 8][:, 0:H * M].rearrange("p (c a m) -> p c a m", a=2, m=M)
                    nc.scalar.copy(dst[0:DH], src[0:DH, :, 0, :])
                    nc.scalar.copy(dst[DH:P], src[DH:P, :, 1, :]).then_inc(turn_taken, 1)
            act.wait_ge(wk_used, WC)
            for q in range(4):
                nc.scalar.mul(a_all[:, 4 * q:4 * q + 4, :], banks[q][:, :].rearrange("p (h n) -> p h n", h=4),
                              DH ** -0.5).then_inc(a_taken, 1)
            nc.scalar.mul(amem[:, :, :], banks[4][:, 0:H * M].rearrange("p (h n) -> p h n", h=H),
                          DH ** -0.5).then_inc(a_taken, 1)
            def take(kind, b, use, dst, src=None):
                act.wait_ge(misc_full, misc_index(kind, b, use) + 1)
                nc.scalar.copy(dst, misc[:, :] if src is None else src).then_inc(misc_free, 1)

            def take_values(kind, b, u, par):
                dst = u_all[:, bass.ds(par, 1), u // 4, 512 * (u % 4):512 * (u % 4 + 1)].squeeze(1)
                take(kind, b, ("U", u), dst)

            def next_xn(kind, b, batches_done):
                act.wait_ge(misc_free, misc_index(kind, b, ("XT",)) + 1)
                at_least(act, scores_full, 4 * H * batches_done)
                nc.scalar.copy(xcur[:, :], xnext[:, :]).then_inc(xcur_ready, 1)

            take("pro", 0, ("XT",), xnext[:, :])
            next_xn("pro", 0, 0)
            act.wait_ge(wo_used, WC)
            for q in range(4):
                nc.scalar.copy(b_all[:, 4 * q:4 * q + 4, :],
                               banks[q][:, :].rearrange("p (h n) -> p h n", h=4)).then_inc(b_taken, 1)
            act.wait_ge(umem_made, 2)
            for half in range(2):
                nc.scalar.copy(umem[:, half, :], banks[4 + half][:, 0:D]).then_inc(b_taken, 1)
            for u in range(16):
                act.wait_ge(u_made, u + 1)
                nc.scalar.copy(u_all[:, 0, u // 4, 512 * (u % 4):512 * (u % 4 + 1)], banks[u % 6][:, :]).then_inc(u_taken, 1)
            take("pro", 0, ("G", H), gT[:, :])

            def take_memory(kind, b, half):
                at_least(act, mem_placed, H * b)
                at_least(act, memmax_ready, b)
                take(kind, b, ("MEM", half), smem[:, 2 * half:2 * half + 2, :, :],
                     misc[:, :].rearrange("p (t h m) -> p t h m", t=2, h=H))

            def batch(kind, b):
                def step(s):
                    g = b * H + s

                    def take_extra(place):
                        use = extra(kind, s, place)
                        if use is None:
                            return
                        if use[0] == "XT":
                            take(kind, b, use, xnext[:, :])
                        elif use[0] == "U":
                            take_values(kind, b, use[1], (b + 1) % 2)
                        elif use[0] == "G":
                            act.wait_ge(gsq_ready, H * (b + 1))
                            take(kind, b, use, gT[:, :])
                        elif use[0] == "MEM":
                            take_memory(kind, b, use[1])
                        elif use[0] == "PM":
                            take(kind, b, use, pmemT[:, use[1], :])
                        elif use[0] == "X1T":
                            take(kind, b, use, x1T[:, :])
                        elif use[0] == "GATE":
                            act.wait_ge(silu_ready, HC * (b - 1) + 1)
                            act.wait_ge(misc_full, misc_index(kind, b, use) + 1)
                            nc.scalar.activation(f_tanh[:, use[1], :], misc[:, :], ACT.Tanh, scale=0.5)
                            nc.scalar.copy(f_gate[:, use[1], :], misc[:, :]).then_inc(misc_free, 1)
                        elif use[0] == "UP":
                            take(kind, b, use, f_up[:, use[1], :])
                        else:
                            act.wait_ge(misc_full, misc_index(kind, b, use) + 1)
                            nc.scalar.mul(ybuf[:, :, :], misc[:, :].rearrange("p (t d) -> p t d", t=T),
                                          0.5).then_inc(misc_free, 1)

                    def count(k):
                        if not lagged(kind, s, k + 1):
                            return
                        at_least(act, first_ready if k == 0 else guess_ready, g if k == 0 else g - 1)
                        act.wait_ge(masked, 4 * (g - k))
                        act.wait_ge(mem_placed, g - k)
                        for p, t in enumerate(ORDER):
                            at_least(act, counted[k], 4 * (g - k - 1) + p)
                            nc.scalar.activation(signs[:, k, 0:ROW[t]], row(scores, ring(head_of(s, k + 1), RING), t),
                                                 ACT.Sign, bias=state[:, s % 2, S_T, k * T + t:k * T + t + 1], scale=-1.0,
                                                 accum_out=counts[:, k * T + t:k * T + t + 1]
                                                 ).then_inc(counted[k], 1)

                    def take_turned(p):
                        if lagged(kind, s, LAG_P):
                            n, t = 4 * (g - LAG_P) + p, ORDER[p]
                            act.wait_ge(t_full, n + 1)
                            at_least(act, pv_done, n - 1)
                            nc.scalar.copy(probsT[:, p % 2, 0:KEYS[t]], t_bank[p % 2][:, 0:KEYS[t]]).then_inc(t_taken, 1)

                    def exponentials(p):
                        if lagged(kind, s, LAG_K):
                            ge, t = g - LAG_K, ORDER[p]
                            if p == 0:
                                act.wait_ge(negmax_ready, ge + 1)
                                at_least(act, probs_ready, 4 * (ge - 1))
                            nc.scalar.activation(row(expo, ring(head_of(s, LAG_K), ERING), t),
                                                 row(scores, ring(head_of(s, LAG_K), RING), t), ACT.Exp,
                                                 bias=negmax[:, bass.ds(ring(head_of(s, LAG_K), RING), 1), t]
                                                 ).then_inc(exp_ready, 1)

                    count(2)
                    if s == LAG_P and kind != "first":
                        act.wait_ge(y_full, b)
                        act.wait_ge(out_sent, 16 * b)
                        nc.scalar.copy(ybuf[:, :, :], y_bank[:, :].rearrange("p (t d) -> p t d", t=T)).then_inc(y_taken, 1)
                    if kind != "drain":
                        take(kind, b, ("SQ", s), gnorm2[:, :], misc[:, 0:T])
                    count(1)
                    take_extra(0)
                    if s == H - 1 and kind in ("first", "mid"):
                        next_xn(kind, b, b + 1)
                    count(0)
                    if kind != "drain" and s < H - 1:
                        act.wait_ge(scores_full, 4 * (g + 1))
                        act.wait_ge(gsq_ready, g + 1)
                        take(kind, b, ("G", s + 1), gT[:, :])
                    exponentials(0)
                    take_turned(0)
                    take_extra(1)
                    exponentials(1)
                    take_turned(1)
                    exponentials(2)
                    take_turned(2)
                    if flagged(kind, s):
                        at_least(act, probs_ready, 4 * (g - LAG_K))
                        take(kind, b, ("FLAG", s), flags[:, :], misc[0:1, 0:T + 1])
                    exponentials(3)
                    take_turned(3)
                    take_extra(2)

                for s in range(H):
                    step(s)

            batches(act, batch)

        @block.vector
        def _(dve):
            nc.vector.memset(minus_half[:, :], -0.5).then_inc(consts_made, 1)
            nc.vector.memset(plus_half[:, :], 0.5).then_inc(consts_made, 1)
            nc.vector.memset(onesP[:, :], 1.0).then_inc(consts_made, 1)
            nc.vector.memset(minus_one[:, :], -1.0).then_inc(consts_made, 1)
            nc.vector.memset(ones[:, :], 1.0).then_inc(consts_made, 1)
            dve.wait_ge(mix_in, 16 * 5)
            for a in range(2):
                nc.vector.tensor_copy(post_x[a * DH:(a + 1) * DH], post_raw[a * DH:(a + 1) * DH].rearrange(
                    "p (h c a) -> p a c h", a=2, c=WC)[:, a]).then_inc(post_spread, 1)
            dve.wait_ge(w_in, 16 * 10)
            for a in range(3):
                nc.vector.tensor_scalar(w_f[:, a], w_int[:, a], 1.0 / 127.0, None, ALU.mult).then_inc(ffn_w_ready, 1)
            dve.wait_ge(turn_taken, 8)
            for c in range(WC):
                if c >= 2:
                    dve.wait_ge(wk_used, c - 1)
                nc.vector.tensor_tensor(wk_mix[:, c % 2], wkT[:, c, :].unsqueeze(1).to_broadcast([P, H, P + M]),
                                        pre_x[:, c, :].unsqueeze(2).to_broadcast([P, H, P + M]),
                                        ALU.mult).then_inc(wk_mixed, 1)

            dve.wait_ge(post_spread, 2)
            nc.vector.tensor_tensor(mv_mix[:, :, :, :], mvT[:, :, :].unsqueeze(2).to_broadcast([P, WC, H, M]),
                                    post_x[:, :, :].unsqueeze(3).to_broadcast([P, WC, H, M]), ALU.mult).then_inc(mv_mixed, 1)

            def norm_stats(kind, b, what, src):
                n = ln_index(kind, b, what)
                for t in range(T):
                    nc.vector.bn_stats(stats[:, t, :], src[:, t, :]).then_inc(ln_stats, 1)
                dve.wait_ge(ln_stats, 4 * (n + 1))
                at_least(dve, ln_out, n)
                alone(dve)
                for t in range(T):
                    nc.vector.bn_aggr(meanvar[:, t, :], stats[:, t, :]).then_inc(ln_meanvar, 1)

            dve.wait_ge(x_in, 16)
            norm_stats("pro", 0, "x", xwork)

            def memory_maxima(kind, b):
                dve.wait_ge(misc_free, misc_index(kind, b, ("MEM", 1)) + 1)
                at_least(dve, masked, 4 * H * b)
                nc.vector.reduce_max(memmax[:, :, :].rearrange("p t h -> p (t h)"),
                                     smem[:, :, :, :].rearrange("p t h m -> p (t h) m"),
                                     AX_X).then_inc(memmax_ready, 1)
                dve.wait_ge(memmax_ready, b + 1)

            def general_kth(slot, t):
                wrk = probs[:, AT[t]:AT[t] + ROW[t]]
                nc.vector.tensor_copy(wrk, row(scores, slot, t)).then_inc(topk_step, 1)
                for i in range(15):
                    dve.wait_ge(topk_step, i + 1)
                    if i % 2 == 0:
                        nc.vector.max(top8[:, :], wrk).then_inc(topk_step, 1)
                    else:
                        nc.vector.match_replace(wrk, top8[:, :], wrk, -FMAX).then_inc(topk_step, 1)
                dve.wait_ge(topk_step, 16)
                nc.vector.tensor_copy(kth[:, slot, t:t + 1], top8[:, 7:8]).then_inc(topk_step, 1)
                dve.wait_ge(topk_step, 17)
                dve.sem_clear(topk_step)

            dve.wait_ge(table_in, 16)
            dve.wait_ge(state_set, 3)

            def batch(kind, b):
                def step(s):
                    g = b * H + s
                    v = nc.vector
                    slot_k, slot_p = ring(head_of(s, LAG_K), RING), ring(head_of(s, LAG_P), RING)
                    gk, gp = g - LAG_K, g - LAG_P
                    selects, applies = lagged(kind, s, LAG_K), lagged(kind, s, LAG_P)
                    moves = any(lagged(kind, s, k + 1) for k in range(GUESSES))
                    old, new = state[:, s % 2], state[:, (s + 1) % 2]

                    if selects:
                        dve.wait_ge(guess_ready, g - 1)
                        v.tensor_copy(cand[:, :, 0:1].squeeze(2),
                                      old[:, S_T, GUESSES * T:(GUESSES + 1) * T]).then_inc(guess_taken, 1)
                    def count_found(p):
                        t = ORDER[p]
                        v.tensor_scalar(work[:, AT[t]:AT[t] + ROW[t]], row(scores, slot_k, t),
                                        cand[:, t, 0:1], None, ALU.is_ge, ALU.add,
                                        accum_out=found[:, t:t + 1]).then_inc(select_step, 1)

                    if selects:
                        dve.wait_ge(mem_placed, gk + 1)
                        dve.wait_ge(masked, 4 * gk + 4)
                        dve.wait_ge(guess_taken, gk + 1)
                        count_found(0)
                        count_found(1)
                    if applies:
                        dve.wait_ge(misc_free, flag_index(kind, b, s) + 1)
                        alone(dve)
                        rows_missed = dve.value_load(flags[0:1, T:T + 1].bitcast(I32), min_val=0, max_val=2 ** 31 - 1)
                    if selects:
                        count_found(2)
                        count_found(3)
                    if applies:
                        dve.wait_ge(exp_ready, 4 * gp + 4)
                        at_least(dve, t_full, 4 * gp)
                        at_least(dve, pmem_ready, gp)
                        at_least(dve, scaled, 4 * gp)
                        dve.wait_ge(kth_ready, gp + 1)
                        alone(dve)
                        with dve.If(rows_missed > 0):
                            for t in range(T):
                                of_tile = dve.value_load(flags[0:1, t:t + 1].bitcast(I32), min_val=0,
                                                         max_val=2 ** 31 - 1)
                                with dve.If(of_tile > 0):
                                    general_kth(slot_p, t)
                        for t in ORDER:
                            v.scalar_tensor_tensor(
                                out=probs[:, AT[t]:AT[t] + ROW[t]], in0=row(scores, slot_p, t),
                                scalar=kth[:, bass.ds(slot_p, 1), t], in1=row(expo, ring(head_of(s, LAG_P), ERING), t),
                                op0=ALU.is_ge, op1=ALU.mult, accum_out=rowsum[:, t:t + 1]).then_inc(probs_ready, 1)
                    if selects:
                        def hide(p):
                            t = ORDER[p]
                            wrk = work[:, AT[t]:AT[t] + ROW[t]]
                            v.scalar_tensor_tensor(out=wrk, in0=wrk, scalar=-FMAX, in1=row(scores, slot_k, t),
                                                   op0=ALU.mult, op1=ALU.add).then_inc(select_step, 1)

                        dve.wait_ge(select_step, T)
                        hide(0)
                    if applies:
                        dve.wait_ge(probs_ready, 4 * gp + 4)
                        v.reciprocal(rinv[:, :], rowsum[:, :]).then_inc(rinv_ready, 1)
                    if selects:
                        v.tensor_tensor(offset[:, :, :], ranks, found[:, :].unsqueeze(2).to_broadcast([P, T, 9]),
                                        ALU.add).then_inc(select_step, 1)
                        v.tensor_scalar(short[:, :], found[:, :], -float(AIM), None, ALU.add).then_inc(select_step, 1)
                        hide(1)
                        dve.wait_ge(select_step, T + 3)
                        v.tensor_tensor(off_aim[:, :], short[:, :], short[:, :], ALU.mult).then_inc(select_step, 1)
                        hide(2)
                        dve.wait_ge(select_step, T + 5)
                        v.scalar_tensor_tensor(out=missed[:, 0:T], in0=off_aim[:, :], scalar=WINDOW ** 2 + 0.5,
                                               in1=active, op0=ALU.is_gt, op1=ALU.mult,
                                               accum_out=missed[:, T:T + 1]).then_inc(bad_ready, 1)
                        hide(3)
                        for p, t in enumerate(ORDER):
                            dve.wait_ge(select_step, T + (1, 4, 6, 7)[p])
                            v.max(cand[:, t, 1:9], work[:, AT[t]:AT[t] + ROW[t]]).then_inc(select_step, 1)

                    def pick_rank():
                        if selects:
                            dve.wait_ge(select_step, 2 * T + 7)
                            v.scalar_tensor_tensor(out=offset[:, :, :], in0=offset[:, :, :], scalar=0.0,
                                                   in1=cand[:, :, :], op0=ALU.is_equal,
                                                   op1=ALU.mult).then_inc(select_step, 1)

                    def pick_value():
                        if selects:
                            dve.wait_ge(select_step, 2 * T + 8)
                            v.tensor_reduce(short[:, :], offset[:, :, :], AX_X, ALU.add).then_inc(select_step, 1)

                    def pick_end():
                        if selects:
                            dve.wait_ge(select_step, 2 * T + 9)
                            dve.sem_clear(select_step)
                            v.tensor_tensor(kth[:, bass.ds(slot_k, 1), :].squeeze(1), short[:, :], cap,
                                            ALU.min).then_inc(kth_ready, 1)

                    if moves:
                        for k in range(GUESSES):
                            if lagged(kind, s, k + 1):
                                dve.wait_ge(counted[k], 4 * (g - k))
                        at_least(dve, first_ready, g if lagged(kind, s, 1) else 0)
                        alone(dve)
                        guess, miss, last = old[:, S_T, 0:ALL], new[:, S_LAST + 1, T:T + ALL], old[:, S_LAST + 1, 0:ALL]
                        other = new[:, S_OTHER:S_OTHER + 2, T:T + ALL]
                        v.tensor_tensor(miss, counts[:, :], aim_sum, ALU.subtract).then_inc(guess_step, 1)
                        v.tensor_tensor(between[:, :, :], old[:, S_LAST:S_LAST + 2, 0:ALL], old[:, S_OTHER:S_OTHER + 2, 0:ALL],
                                        ALU.subtract).then_inc(guess_step, 1)
                        v.tensor_copy(new[:, S_LAST, T:T + ALL], guess).then_inc(guess_step, 1)
                        dve.wait_ge(guess_step, 1)
                        v.tensor_tensor(cross[:, :], miss, last, ALU.mult).then_inc(guess_step, 1)
                        v.tensor_tensor(miss2[:, :], miss, miss, ALU.mult).then_inc(guess_step, 1)
                    pick_rank()
                    if moves:
                        dve.wait_ge(guess_step, 4)
                        v.scalar_tensor_tensor(out=between[:, :, :], in0=cross[:, :].unsqueeze(1).to_broadcast([P, 2, ALL]),
                                               scalar=0.0, in1=between[:, :, :], op0=ALU.is_lt,
                                               op1=ALU.mult).then_inc(guess_step, 1)
                        dve.wait_ge(guess_step, 5)
                        v.scalar_tensor_tensor(out=miss2[:, :], in0=miss2[:, :], scalar=(2 * WINDOW + 0.25) ** 2 + 1.0,
                                               in1=miss, op0=ALU.is_gt, op1=ALU.mult).then_inc(guess_step, 1)
                        dve.wait_ge(guess_step, 6)
                        v.tensor_tensor(other, old[:, S_OTHER:S_OTHER + 2, 0:ALL], between[:, :, :],
                                        ALU.add).then_inc(guess_step, 1)
                    pick_value()
                    if moves:
                        dve.wait_ge(guess_step, 8)
                        v.tensor_tensor(over[:, :], miss, other[:, 1], ALU.subtract).then_inc(guess_step, 1)
                        v.tensor_tensor(move[:, :], guess, other[:, 0], ALU.subtract).then_inc(guess_step, 1)
                        dve.wait_ge(guess_step, 9)
                        v.reciprocal(over[:, :], over[:, :]).then_inc(guess_step, 1)
                        dve.wait_ge(guess_step, 10)
                        v.tensor_tensor(move[:, :], move[:, :], miss2[:, :], ALU.mult).then_inc(guess_step, 1)
                    pick_end()
                    if moves:
                        dve.wait_ge(guess_step, 12)
                        v.tensor_tensor(move[:, :], move[:, :], over[:, :], ALU.mult).then_inc(guess_step, 1)
                        dve.wait_ge(guess_step, 13)
                        dve.sem_clear(guess_step)
                        v.tensor_tensor(new[:, S_T, T:T + ALL], guess, move[:, :], ALU.subtract).then_inc(guess_ready, 1)
                    if kind != "drain":
                        if s == 0:
                            memory_maxima(kind, b)
                        slot = ring(s, RING)
                        for p, t in enumerate(ORDER):
                            dve.wait_ge(scores_full, 4 * g + p + 1)
                            v.tensor_scalar(keys(scores, slot, t), s_bank[p][:, 0:KEYS[t]], 1.0,
                                            memmax[:, t, bass.ds(s, 1)], ALU.mult, ALU.max,
                                            accum_out=rowmax[:, bass.ds(slot, 1), t]).then_inc(masked, 1)
                    if kind in ("first", "mid"):
                        if s == 0:
                            dve.wait_ge(x_in, 16 * (b + 2))
                            norm_stats(kind, b, "x", xwork)
                    if kind == "first":
                        return
                    if s == 5:
                        dve.wait_ge(y_taken, b)
                        norm_stats(kind, b, "Y", ybuf)
                    if s == 7:
                        dve.wait_ge(x1_ready, b)
                        norm_stats(kind, b, "X1", xres)
                    if 11 <= s < 11 + HC:
                        c = s - 11
                        dve.wait_ge(silu_pool, HC * (b - 1) + c + 1)
                        v.scalar_tensor_tensor(out=f_up[:, c, :], in0=f_tanh[:, c, :], scalar=1.0,
                                               in1=f_up[:, c, :], op0=ALU.add, op1=ALU.mult).then_inc(silu_ready, 1)
                    if s == 14:
                        dve.wait_ge(misc_free, misc_index(kind, b, ("DOWN",)) + 1)
                        norm_stats(kind, b, "Z", ybuf)

                for s in range(H):
                    step(s)

            batches(dve, batch)

        @block.gpsimd
        def _(pool):
            nc.gpsimd.memset(ident[:, :], 0.0).then_inc(ident_made, 1)
            pool.wait_ge(ident_made, 1)
            nc.gpsimd.affine_select(out=ident[:, :], in_=ident[:, :], compare_op=ALU.not_equal, fill=1.0, base=0,
                                    pattern=[[-1, P]], channel_multiplier=1).then_inc(ident_made, 1)
            nc.gpsimd.memset(causal[:, :], 0.0).then_inc(causal_made, 1)
            pool.wait_ge(causal_made, 1)
            nc.gpsimd.affine_select(out=causal[:, :], in_=causal[:, :], compare_op=ALU.is_ge, fill=MASKED,
                                    base=0, pattern=[[-1, P]], channel_multiplier=1).then_inc(causal_made, 1)
            pool.wait_ge(ident_made, 2)
            nc.gpsimd.tensor_copy(ident16[:, :], ident[:, :]).then_inc(causal_made, 1)
            pool.wait_ge(mix_in, 16 * 5)
            pool.wait_ge(post_spread, 2)
            def norm(kind, b, what, dst, src):
                n = ln_index(kind, b, what)
                pool.wait_ge(ln_meanvar, 4 * (n + 1))
                at_least(pool, ln_out, n)
                alone(pool)
                nc.gpsimd.tensor_scalar(vareps[:, :], meanvar[:, :, 1:2].squeeze(2), EPS, None, ALU.add).then_inc(ln_vareps, 1)
                pool.wait_ge(ln_vareps, n + 1)
                alone(pool)
                nc.gpsimd.tensor_tensor(rstd[:, :], vareps[:, :], minus_half[:, :], ALU.pow).then_inc(ln_rstd, 1)
                pool.wait_ge(ln_rstd, n + 1)
                alone(pool)
                nc.gpsimd.tensor_tensor(dst[:, :, :], src[:, :, :], meanvar[:, :, 0:1].to_broadcast([P, T, D]),
                                        ALU.subtract).then_inc(ln_centred, 1)
                pool.wait_ge(ln_centred, n + 1)
                alone(pool)
                nc.gpsimd.tensor_tensor(dst[:, :, :], dst[:, :, :], rstd[:, :].unsqueeze(2).to_broadcast([P, T, D]),
                                        ALU.mult).then_inc(ln_out, 1)

            def add_residual(kind, b, what, dst, done):
                pool.wait_ge(ln_out, ln_index(kind, b, what) + 1)
                alone(pool)
                nc.gpsimd.tensor_tensor(dst[:, :, :], xres[:, :, :], ybuf[:, :, :], ALU.add).then_inc(done, 1)

            def mix_wo(c):
                if c >= 2:
                    pool.wait_ge(wo_used, c - 1)
                nc.gpsimd.tensor_tensor(wo_mix[:, c % 2], wo_s[:, c, :].unsqueeze(1).to_broadcast([P, H, D]),
                                        post_x[:, c, :].unsqueeze(2).to_broadcast([P, H, D]),
                                        ALU.mult).then_inc(wo_mixed, 1)

            mix_wo(0)
            mix_wo(1)
            nc.gpsimd.memset(state[:, :, :, :], 0.0).then_inc(state_set, 1)
            nc.gpsimd.memset(counts[:, :], 0.0).then_inc(state_set, 1)
            pool.wait_ge(state_set, 2)
            nc.gpsimd.memset(state[:, :, S_OTHER + 1, 0:T], -FAR).then_inc(state_set, 1)
            pool.wait_ge(state_set, 3)
            pool.wait_ge(consts_made, 5)
            norm("pro", 0, "x", xwork, xwork)
            for c in range(2, WC):
                mix_wo(c)
            pool.wait_ge(a_taken, 4)
            nc.gpsimd.tensor_copy(a_now[:, :], a_all[:, 0, :]).then_inc(a_ready, 1)
            pool.wait_ge(table_in, 16)

            def next_a(kind, b, made, after):
                pool.wait_ge(misc_full, misc_index(kind, b, ("G", made)) + 1)
                alone(pool)
                nc.gpsimd.tensor_copy(a_now[:, :], a_all[:, bass.ds(after % H, 1), :].squeeze(1)).then_inc(a_ready, 1)

            def squares(kind, b, made):
                pool.wait_ge(misc_free, misc_index(kind, b, ("G", made)) + 1)
                alone(pool)
                nc.gpsimd.tensor_tensor(gsq[:, :], gT[:, :], gT[:, :], ALU.mult).then_inc(gsq_ready, 1)

            next_a("pro", 0, H, 1)
            squares("pro", 0, H)

            def batch(kind, b):
                def step(s):
                    g = b * H + s
                    if lagged(kind, s, 1):
                        gn = g - 1
                        pool.wait_ge(masked, 4 * gn + 4)
                        alone(pool)
                        slot = ring(head_of(s, 1), RING)
                        nc.gpsimd.tensor_tensor(negmax[:, bass.ds(slot, 1), :].squeeze(1),
                                                rowmax[:, bass.ds(slot, 1), :].squeeze(1), minus_one[:, :],
                                                ALU.mult).then_inc(negmax_ready, 1)
                    if kind != "drain":
                        pool.wait_ge(misc_free, misc_index(kind, b, ("SQ", s)) + 1)
                        at_least(pool, first_ready, g)
                        alone(pool)
                        nc.gpsimd.tensor_tensor(gnorm[:, :], gnorm2[:, :], plus_half[:, :], ALU.pow).then_inc(gnorm_step, 1)
                    if lagged(kind, s, LAG_P):
                        gp = g - LAG_P
                        pool.wait_ge(rinv_ready, gp + 1)
                        at_least(pool, probs_ready, 4 * gp + 4)
                        alone(pool)
                        for t in ORDER:
                            prb = probs[:, AT[t]:AT[t] + ROW[t]]
                            nc.gpsimd.tensor_scalar(prb, prb, rinv[:, t:t + 1], 1.0, ALU.mult,
                                                    ALU.mult).then_inc(scaled, 1)
                        if s == LAG_P and kind != "first":
                            pool.wait_ge(misc_full, misc_index(kind, b, ("PM", 1)) + 1)
                        pool.wait_ge(scaled, 4 * gp + 4)
                        alone(pool)
                        nc.gpsimd.tensor_copy(head_mem(pmem, head_of(s, LAG_P)), mem_parts(probs[:, :])).then_inc(pmem_ready, 1)
                    if kind != "drain":
                        if s == 0:
                            pool.wait_ge(misc_free, misc_index(kind, b, ("MEM", 1)) + 1)
                        slot = ring(head_of(s, 0), RING)
                        if kind != "first" or s >= RING:
                            pool.wait_ge(probs_ready, 4 * (g - RING + 1))
                        alone(pool)
                        nc.gpsimd.tensor_copy(mem_parts(scores[:, bass.ds(slot, 1), :].squeeze(1)),
                                              head_mem(smem, s)).then_inc(mem_placed, 1)
                    if kind != "drain" and not (kind == "last" and s == H - 1):
                        next_a(kind, b, s + 1, s + 2)
                        squares(kind, b, s + 1)
                    if kind != "drain":
                        pool.wait_ge(gnorm_step, 1)
                        at_least(pool, guess_ready, g - 1)
                        alone(pool)
                        new = state[:, (s + 1) % 2]
                        nc.gpsimd.tensor_tensor(new[:, S_OTHER, 0:T], gnorm[:, :], far_point, ALU.mult).then_inc(gnorm_step, 1)
                        pool.wait_ge(gnorm_step, 2)
                        pool.sem_clear(gnorm_step)
                        nc.gpsimd.tensor_tensor(new[:, S_T, 0:T], gnorm[:, :], first_guess, ALU.mult).then_inc(first_ready, 1)
                    extras(kind, b, s)

                def extras(kind, b, s):
                    if s == 1 and kind in ("first", "mid"):
                        norm(kind, b, "x", xwork, xwork)
                    if kind == "first":
                        return
                    if s == 6:
                        norm(kind, b, "Y", ybuf, ybuf)
                        pool.wait_ge(res_in, 16 * b)
                        add_residual(kind, b, "Y", xres, x1_ready)
                    if s == 8:
                        if kind == "mid":
                            pool.wait_ge(misc_full, misc_index(kind, b, ("XT",)) + 1)
                        norm(kind, b, "X1", xwork, xres)
                    if 11 <= s < 11 + HC:
                        c = s - 11
                        pool.wait_ge(misc_free, misc_index(kind, b, ("UP", c)) + 1)
                        alone(pool)
                        nc.gpsimd.tensor_tensor(f_up[:, c, :], f_up[:, c, :], f_gate[:, c, :], ALU.mult).then_inc(silu_pool, 1)
                    if s == 15:
                        norm(kind, b, "Z", ybuf, ybuf)
                        add_residual(kind, b, "Z", ybuf, out_ready)

                for s in range(H):
                    step(s)

            batches(pool, batch)


_INS = ['L0_attn_x', 'L0_attn_Wq', 'L0_attn_Wk', 'L0_attn_Wv', 'L0_attn_pre_proj', 'L0_attn_post_proj',
        'L0_attn_mem_k', 'L0_attn_mem_v', 'L0_attn_Wo', 'L0_attn_bo', 'L0_ffn_w_gate', 'L0_ffn_w_up',
        'L0_ffn_w_down']
_OUTS = [((B, N, D), 'float32')]


def kernel(**inputs):
    import numpy as _np
    import concourse.bacc as _bacc
    from concourse import mybir as _mybir
    from concourse.bass_utils import run_bass_kernel_spmd as _run

    nc = _bacc.Bacc("TRN2", target_bir_lowering=False, num_devices=1)
    arrays, args = {}, []
    table = guess_table()
    arrays["in_guess_table_dram"] = table
    args.append(nc.dram_tensor("in_guess_table_dram", table.shape, F32, kind="ExternalInput").ap())
    for name in _INS:
        a = _np.ascontiguousarray(inputs[name])
        arrays[f"in_{name}_dram"] = a
        args.append(nc.dram_tensor(f"in_{name}_dram", a.shape, _mybir.dt.from_np(a.dtype), kind="ExternalInput").ap())
    for i, (shape, dtype) in enumerate(_OUTS):
        dt = _mybir.dt.from_np(_np.dtype(dtype))
        args.append(nc.dram_tensor(f"out_{i}_dram", shape, dt, kind="ExternalOutput").ap())
    build(nc, *args)
    r = _run(nc, [arrays], core_ids=[0])
    got = tuple(r.results[0][f"out_{i}_dram"] for i in range(len(_OUTS)))
    return got[0]
```
